# Optimizing a Trainium2 kernel written in Bass

```python
import numpy as np
import jax
import jax.numpy as jnp

def _softmax(x, axis=-1):
    return jax.nn.softmax(x, axis=axis)

def _gelu(x):
    return jax.nn.gelu(x, approximate=True)

def _silu(x):
    return jax.nn.silu(x)

def _sigmoid(x):
    return jax.nn.sigmoid(x)

def _layernorm(x, axis=-1, eps=1e-05):
    m = jnp.mean(x, axis=axis, keepdims=True)
    v = jnp.var(x, axis=axis, keepdims=True)
    return (x - m) / jnp.sqrt(v + eps)

def _scatter_add(tgt, idx, src, axis=0):
    return tgt.at[idx].add(src)

def _segment_sum(src, seg, n):
    return jax.ops.segment_sum(src, seg, n)
kernel_name = 'mk_prb_d2_jaxref_r8_bfdfcd'

def setup_inputs(seed: int=0):
    np.random.seed(seed)
    _w = jnp.asarray

    def _L0_attn_setup():
        import jax, jax.numpy as jnp
        import numpy as np
        HEAD_NUM = 16
        ROPE_BASE = 10000.0

        def _rotate_half(x):
            x_even = x[..., ::2]
            x_odd = x[..., 1::2]
            return jnp.stack((-x_odd, x_even), axis=-1).reshape(x.shape)

        def _rope_cos_sin(seq_len, head_dim):
            half = head_dim // 2
            inv_freq = 1.0 / ROPE_BASE ** (jnp.arange(half, dtype=jnp.float32) / half)
            t = jnp.arange(seq_len, dtype=jnp.float32)
            freqs = t[:, None] * inv_freq[None, :]
            cos = jnp.repeat(jnp.cos(freqs), 2, axis=-1)
            sin = jnp.repeat(jnp.sin(freqs), 2, axis=-1)
            return (cos, sin)
        key = jax.random.key(seed)
        ks = jax.random.split(key, 9)
        B, S, H = (2, 256, 256)
        std = 1.0 / np.sqrt(H)
        return {'x': jax.random.normal(ks[0], (B, S, H), jnp.float32), 'Wq': jax.random.normal(ks[1], (H, H), jnp.float32) * std, 'bq': jax.random.normal(ks[2], (H,), jnp.float32) * std, 'Wk': jax.random.normal(ks[3], (H, H), jnp.float32) * std, 'bk': jax.random.normal(ks[4], (H,), jnp.float32) * std, 'Wv': jax.random.normal(ks[5], (H, H), jnp.float32) * std, 'bv': jax.random.normal(ks[6], (H,), jnp.float32) * std, 'Wo': jax.random.normal(ks[7], (H, H), jnp.float32) * std, 'bo': jax.random.normal(ks[8], (H,), jnp.float32) * std}
    _L0_attn_in = _L0_attn_setup()

    def _L0_ffn_setup():
        import jax, jax.numpy as jnp
        import numpy as np
        TOPK = 2
        key = jax.random.key(seed)
        ks = jax.random.split(key, 6)
        B, T, H, S, r, ad = (2, 512, 256, 32, 16, 32)
        h = jax.random.normal(ks[0], (B, T, H), dtype=jnp.float32)
        Wr = jax.random.normal(ks[1], (S, H), dtype=jnp.float32) * 0.02
        U = jax.random.normal(ks[2], (S, H, r), dtype=jnp.float32) * 0.02
        V = jax.random.normal(ks[3], (S, r, H), dtype=jnp.float32) * 0.02
        attr = jax.random.normal(ks[4], (S, ad), dtype=jnp.float32) * 0.02
        Wa = jax.random.normal(ks[5], (1, ad), dtype=jnp.float32) * 0.02
        return {'h': h, 'Wr': Wr, 'U': U, 'V': V, 'attr': attr, 'Wa': Wa}
    _L0_ffn_in = _L0_ffn_setup()

    def _L1_attn_setup():
        import jax, jax.numpy as jnp
        import numpy as np
        HEADS = 16
        key = jax.random.key(seed)
        ks = jax.random.split(key, 5)
        B, T, D = (2, 256, 256)
        s = 0.02
        return {'x': jax.random.normal(ks[0], (B, T, D), dtype=jnp.float32), 'Wq': jax.random.normal(ks[1], (D, D), dtype=jnp.float32) * s, 'Wk': jax.random.normal(ks[2], (D, D), dtype=jnp.float32) * s, 'Wv': jax.random.normal(ks[3], (D, D), dtype=jnp.float32) * s, 'Wo': jax.random.normal(ks[4], (D, D), dtype=jnp.float32) * s}
    _L1_attn_in = _L1_attn_setup()

    def _L1_ffn_setup():
        import jax, jax.numpy as jnp
        import numpy as np
        D_IN = 256
        D_OUT = 256
        EPS = 1e-05
        key = jax.random.key(seed)
        k_x, k_w = jax.random.split(key)
        x = jax.random.normal(k_x, (8, 256, D_IN), dtype=jnp.float32)
        weight = jax.random.normal(k_w, (D_OUT, D_IN), dtype=jnp.float32)
        gamma = jnp.ones((D_OUT,), dtype=jnp.float32)
        beta = jnp.zeros((D_OUT,), dtype=jnp.float32)
        ln_weight = jnp.ones((D_IN,), dtype=jnp.float32)
        ln_bias = jnp.zeros((D_IN,), dtype=jnp.float32)
        return {'x': x, 'weight': weight, 'gamma': gamma, 'beta': beta, 'ln_weight': ln_weight, 'ln_bias': ln_bias}
    _L1_ffn_in = _L1_ffn_setup()
    _d = {'L0_attn_x': _L0_attn_in['x'], 'L0_attn_Wq': _L0_attn_in['Wq'], 'L0_attn_bq': _L0_attn_in['bq'], 'L0_attn_Wk': _L0_attn_in['Wk'], 'L0_attn_bk': _L0_attn_in['bk'], 'L0_attn_Wv': _L0_attn_in['Wv'], 'L0_attn_bv': _L0_attn_in['bv'], 'L0_attn_Wo': _L0_attn_in['Wo'], 'L0_attn_bo': _L0_attn_in['bo'], 'L0_ffn_Wr': _L0_ffn_in['Wr'], 'L0_ffn_U': _L0_ffn_in['U'], 'L0_ffn_V': _L0_ffn_in['V'], 'L0_ffn_attr': _L0_ffn_in['attr'], 'L0_ffn_Wa': _L0_ffn_in['Wa'], 'L1_attn_Wq': _L1_attn_in['Wq'], 'L1_attn_Wk': _L1_attn_in['Wk'], 'L1_attn_Wv': _L1_attn_in['Wv'], 'L1_attn_Wo': _L1_attn_in['Wo'], 'L1_ffn_weight': _L1_ffn_in['weight'], 'L1_ffn_gamma': _L1_ffn_in['gamma'], 'L1_ffn_beta': _L1_ffn_in['beta'], 'L1_ffn_ln_weight': _L1_ffn_in['ln_weight'], 'L1_ffn_ln_bias': _L1_ffn_in['ln_bias']}
    _x0 = _d['L0_attn_x']
    _d['L0_attn_x'] = jax.random.normal(jax.random.fold_in(jax.random.key(seed), 1), (4, 1024, 256), dtype=_x0.dtype)
    del _x0
    return _d

def reference(L0_attn_x, L0_attn_Wq, L0_attn_bq, L0_attn_Wk, L0_attn_bk, L0_attn_Wv, L0_attn_bv, L0_attn_Wo, L0_attn_bo, L0_ffn_Wr, L0_ffn_U, L0_ffn_V, L0_ffn_attr, L0_ffn_Wa, L1_attn_Wq, L1_attn_Wk, L1_attn_Wv, L1_attn_Wo, L1_ffn_weight, L1_ffn_gamma, L1_ffn_beta, L1_ffn_ln_weight, L1_ffn_ln_bias):

    def _L0_attn_ref(x, Wq, bq, Wk, bk, Wv, bv, Wo, bo):
        import jax, jax.numpy as jnp
        import numpy as np
        HEAD_NUM = 16
        ROPE_BASE = 10000.0

        def _rotate_half(x):
            x_even = x[..., ::2]
            x_odd = x[..., 1::2]
            return jnp.stack((-x_odd, x_even), axis=-1).reshape(x.shape)

        def _rope_cos_sin(seq_len, head_dim):
            half = head_dim // 2
            inv_freq = 1.0 / ROPE_BASE ** (jnp.arange(half, dtype=jnp.float32) / half)
            t = jnp.arange(seq_len, dtype=jnp.float32)
            freqs = t[:, None] * inv_freq[None, :]
            cos = jnp.repeat(jnp.cos(freqs), 2, axis=-1)
            sin = jnp.repeat(jnp.sin(freqs), 2, axis=-1)
            return (cos, sin)
        B, S, H = x.shape
        nh = HEAD_NUM
        d = H // nh
        scale = jnp.float32(np.sqrt(d))

        def proj(W, b):
            y = x @ W.T + b
            return y.reshape(B, S, nh, d).transpose(0, 2, 1, 3)
        Q = proj(Wq, bq)
        K = proj(Wk, bk)
        V = proj(Wv, bv)
        cos, sin = _rope_cos_sin(S, d)
        Q = Q * cos + _rotate_half(Q) * sin
        K = K * cos + _rotate_half(K) * sin
        scores = jnp.einsum('bhqd,bhkd->bhqk', Q, K) / scale
        causal = jnp.tril(jnp.ones((S, S), dtype=bool))
        scores = jnp.where(causal, scores, jnp.float32(-jnp.inf))
        attn = jax.nn.softmax(scores, axis=-1)
        out = jnp.einsum('bhqk,bhkd->bhqd', attn, V)
        out = out.transpose(0, 2, 1, 3).reshape(B, S, H)
        return out @ Wo.T + bo

    def _L0_ffn_ref(h, Wr, U, V, attr, Wa):
        import jax, jax.numpy as jnp
        import numpy as np
        TOPK = 2
        S = Wr.shape[0]
        sc = jnp.einsum('bth,sh->bts', h, Wr)
        _, idx = jax.lax.top_k(sc, TOPK)
        m = jax.nn.one_hot(idx, S, dtype=sc.dtype).sum(axis=-2)
        g = jax.nn.softmax(sc, axis=-1) * m
        g = g / (g.sum(axis=-1, keepdims=True) + 1e-08)
        hU = jnp.einsum('bth,shr->btsr', h, U)
        out = jnp.einsum('bts,btsr,srh->bth', g, hU, V)
        aw = jax.nn.sigmoid(attr @ Wa[0])
        gate = (g @ aw)[..., None]
        return out * (0.9 + 0.2 * gate)

    def _L1_attn_ref(x, Wq, Wk, Wv, Wo):
        import jax, jax.numpy as jnp
        import numpy as np
        HEADS = 16
        B, T, _ = x.shape
        H = HEADS
        Dh = Wq.shape[1] // H
        q = (x @ Wq).reshape(B, T, H, Dh)
        k = (x @ Wk).reshape(B, T, H, Dh)
        v = (x @ Wv).reshape(B, T, H, Dh)
        scores = jnp.einsum('bthd,bshd->bhts', q, k)
        mask = jnp.tril(jnp.ones((T, T), dtype=scores.dtype))
        scores = scores * mask
        attn = jax.nn.softmax(scores / T ** 0.5, axis=-1)
        out = jnp.einsum('bhts,bshd->bthd', attn, v).reshape(B, T, H * Dh)
        return out @ Wo

    def _L1_ffn_ref(x, weight, gamma, beta, ln_weight, ln_bias):
        import jax, jax.numpy as jnp
        import numpy as np
        D_IN = 256
        D_OUT = 256
        EPS = 1e-05
        mean = jnp.mean(x, axis=-1, keepdims=True)
        var = jnp.mean(jnp.square(x - mean), axis=-1, keepdims=True)
        xn = (x - mean) * jax.lax.rsqrt(var + EPS) * ln_weight + ln_bias
        quant_w = jnp.sign(weight)
        scale = jnp.max(jnp.abs(weight))
        out = jnp.einsum('bsk,ok->bso', xn, quant_w)
        return out * scale * gamma + beta
    x = L0_attn_x
    xn = _layernorm(x, axis=-1)
    x = x + _L0_attn_ref(xn, L0_attn_Wq, L0_attn_bq, L0_attn_Wk, L0_attn_bk, L0_attn_Wv, L0_attn_bv, L0_attn_Wo, L0_attn_bo) + _L0_ffn_ref(xn, L0_ffn_Wr, L0_ffn_U, L0_ffn_V, L0_ffn_attr, L0_ffn_Wa)
    xn = _layernorm(x, axis=-1)
    x = x + _L1_attn_ref(xn, L1_attn_Wq, L1_attn_Wk, L1_attn_Wv, L1_attn_Wo) + _L1_ffn_ref(xn, L1_ffn_weight, L1_ffn_gamma, L1_ffn_beta, L1_ffn_ln_weight, L1_ffn_ln_bias)
    return x

_drawn_inputs = setup_inputs


def setup_inputs(seed=0):
    import zlib

    import numpy as np

    out = dict(_drawn_inputs(seed))
    spreads = {'L1_ffn_gamma': (1.0, 0.2),
     'L1_ffn_beta': (0.0, 2.0),
     'L1_ffn_ln_weight': (1.0, 0.2),
     'L1_ffn_ln_bias': (0.0, 0.1)}
    factors = {'L0_attn_bq': 7.937,
     'L0_attn_bk': 8.0,
     'L0_ffn_Wr': 3.328,
     'L0_ffn_U': 3.235,
     'L0_ffn_V': 3.214,
     'L0_ffn_attr': 64.0,
     'L0_ffn_Wa': 64.0,
     'L1_attn_Wq': 64.0,
     'L1_attn_Wk': 64.0,
     'L1_attn_Wv': 47.469,
     'L1_attn_Wo': 48.584}
    for name, (base, spread) in spreads.items():
        noise = np.random.default_rng([zlib.crc32(name.encode()), seed]).standard_normal(out[name].shape)
        drawn = base * np.exp(spread * noise) if base else spread * noise
        out[name] = jnp.asarray(drawn.astype(out[name].dtype))
    for name, factor in factors.items():
        out[name] = (out[name] * factor).astype(out[name].dtype)
    return out
```

```python
import concourse.bass as bass
from concourse import mybir
from contextlib import ExitStack
import numpy as np

F32 = mybir.dt.float32
BF16 = mybir.dt.bfloat16
ALU = mybir.AluOpType
ACT = mybir.ActivationFunctionType
AX = mybir.AxisListType

P = 128
B, T, D = 4, 1024, 256
HEADS, DH = 16, 16
NT = T // P
KC = D // P
GH = 4
NG = HEADS // GH
SLOTS, RANK = 32, 16
FF = SLOTS * RANK
FC = FF // P
VA = DH + 1
HC = P // DH
EPS = 1e-5
Q_PARTS = (0, 0, 1, 0, 2, 1)
K_PARTS = (0, 1, 0, 2, 0, 1)
KR = len(Q_PARTS) * DH
KM = KR + 3
BIG = 3.0e38
SCALE = (1.0 / np.sqrt(DH), 1.0 / np.sqrt(T))

def max_units():
    out = []
    for qb in range(NT):
        for seg in range(1 if qb < 4 else 2):
            w = 512 if seg == 0 and qb >= 4 else (qb % 4 + 1) * P
            n = min(512 // w, GH)
            if qb == 0:
                n = 2
            out += [(seg, qb, j, n, w, seg == 1 or qb < 4) for j in range(0, GH, n)]
    return out


def exp_units():
    out = []
    for kb in range(NT):
        n = 1 if kb < 4 else (2 if kb < 6 else 4)
        out += [(kb, j, n) for j in range(0, GH, n)]
    return out


MAXU, EXPU = max_units(), exp_units()
NMX, NEX = len(MAXU), len(EXPU)
RING = NMX + 3
RING_TURN = NG * RING
assert RING % 2 == 0 and NEX % 2 == 0 and (NMX + 1) % 2 == 0


def stage_units(layer):
    u = [(("xT", i), "act") for i in range(NT // 2)]
    kinds = ("q", "qs", "k", "ks") if layer == 0 else ("q", "k")
    u += [((kind, ot, hf), "dve") for ot in range(KC) for hf in range(2) for kind in kinds]
    u += [(("v", i), "dve") for i in range(NT // 2)]
    if layer == 0:
        u += [(("router", 0), "dve")]
        for n in range(NT + 2):
            if n < NT:
                u += [(("hU", n), "dve")]
            if 1 <= n <= NT:
                u += [(("gT", n - 1), "act")]
            if n >= 2:
                u += [(("ffn", n - 2), "dve")]
    else:
        u += [(("x2T", i), "act") for i in range(NT // 2)]
        u += [(("ffn", i), "dve") for i in range(NT // 2)]
        u += [(("later", n), "dve") for n in range(NT - 1, -1, -1)]
    n_before = len(u)
    for i in range(NT // 2):
        u += [(("aT", i), "act")]
        u += [(("wo", i - 1), "dve")] if i else []
    u += [(("wo", NT // 2 - 1), "dve")]
    return u, n_before


class Signal:

    def __init__(self, sem, per, credit=0, step=1):
        self.sem, self.per, self.credit, self.step = sem, per, credit, step

    def count(self, turn, n):
        return (turn * self.per + (n + self.credit)) * self.step


def wait_apart(eng, sem, count, spare):
    eng.wait_ge(sem, count)
    eng.sem_inc(spare, 1)


class Chain:

    def __init__(self, eng, mark, turn):
        self.eng, self.mark, self.turn, self.n = eng, mark, turn, 0

    def __call__(self, instruction):
        self.n += 1
        instruction.then_inc(self.mark.sem, 1)
        self.eng.wait_ge(self.mark.sem, self.mark.count(self.turn, self.n))

    def close(self):
        assert self.n == self.mark.per, (self.n, self.mark.per)


def build(nc, a, out):
    ctx = ExitStack()
    nc.disable_value_cache = True
    with ctx:
        def sb(name, shape, dt=F32):
            return ctx.enter_context(nc.sbuf_tensor(name, shape, dt))

        def sem(name):
            return ctx.enter_context(nc.semaphore(name))

        QS = sb("QS", [P, HEADS * T], BF16)
        KS = sb("KS", [P, HEADS * T], BF16)
        PTb = sb("PTb", [P, 2 * GH * T])
        PT = PTb[:, :].rearrange("p (s h q) -> p s h q", s=2, h=GH)
        rope_a = PTb[:, 0:1024].rearrange("p (s n) -> p s n", s=2)
        rope_b = PTb[:, 1024:2048].rearrange("p (s n) -> p s n", s=2)
        proj = PTb[:, 2048:3072].rearrange("p (s n) -> p s n", s=2)
        rest = PTb[:, 3072:4096].rearrange("p (s n) -> p s n", s=2)
        gh = PTb[:, 4096:5120].rearrange("p (s n) -> p s n", s=2)
        ghT = PTb[:, 5120:6144].rearrange("p (s c n) -> p s c n", s=2, c=FC)
        suffix = PTb[:, 4096:4096 + 6 * HEADS * VA].rearrange("p (n c) -> p n c", n=6)
        xn = PTb[:, 6144:8192].rearrange("p (n d) -> p n d", n=NT)
        RA = sb("RA", [P, 6144])
        parts = RA[:, :].bitcast(BF16).rearrange("p (i k o q) -> p i k o q", i=3, k=2, o=KC)
        OT = RA[:, 0:T]
        attn = RA[:, 1024:3072].rearrange("p (n d) -> p n d", n=NT)
        attnT = RA[:, 3072:5120].rearrange("p (c t) -> p c t", c=KC)
        x = sb("x", [P, NT, D])
        xT = sb("xT", [P, KC, T])
        y = xT[:, :, :].rearrange("p c t -> p (c t)").rearrange("p (n d) -> p n d", n=NT)
        Vaug = sb("Vaug", [P, NT * HEADS * VA])
        Vst = sb("Vst", [P, NT, GH * 32])
        later_v = sb("later_v", [P, HEADS * NT * VA])
        ev = RA[:, 5120:5120 + GH * NT * VA]
        e_all = sb("e_all", [P, HEADS * NT])
        num = RA[:, 5700:5700 + 4 * GH * VA].rearrange("p (n h c) -> p n h c", n=4, h=GH)
        rec = sb("rec", [P, 4, GH])
        mxa = sb("mxa", [P, GH, NT])
        mxb = sb("mxb", [P, GH, 4])
        floor = sb("floor", [P, GH, NT])
        mrest = sb("mrest", [P, GH * NT])
        nmp = sb("nmp", [P, 3, GH * NT], BF16)
        nmT = sb("nmT", [P, P], BF16)
        stats = sb("stats", [P, NT, 6])
        mv = sb("mv", [P, NT, 2])
        rstd = sb("rstd", [P, NT])
        veps = sb("veps", [P, NT])
        std = sb("std", [P, NT])
        sc = later_v[:, 0:NT * SLOTS].rearrange("p (n s) -> p n s", n=NT)
        top8 = sb("top8", [P, NT, 8])
        pre = later_v[:, 512:1536].rearrange("p (i n s) -> p i n s", i=2, n=NT)
        r1 = later_v[:, 256:512].rearrange("p (n s) -> p n s", n=NT)
        r2 = sb("r2", [P, NT, SLOTS])
        rc = sb("rc", [P, 6, NT])
        awb = sb("awb", [P, SLOTS])
        ident = sb("ident", [P, P])
        identb = sb("identb", [P, P], BF16)
        negmask = sb("negmask", [P, P], BF16)
        negmaskT = sb("negmaskT", [P, P], BF16)
        strict = sb("strict", [P, P])
        ones = sb("ones", [P, P])
        w = {n: sb("w_" + n, [P, KC, D]) for n in
             ("q0", "qs0", "k0", "ks0", "v0", "o0", "q1", "k1", "v1", "o1", "f1")}
        w_r = sb("w_r", [P, KC, SLOTS])
        w_u = sb("w_u", [P, KC, FF])
        w_v = sb("w_v", [P, FC, D])
        cos = sb("cos", [P, T])
        sin = sb("sin", [P, T])
        bcol = sb("bcol", [P, 4, KC])
        lncol = sb("lncol", [P, 2, KC])
        brow = sb("brow", [P, 4, D])
        attrT = sb("attrT", [SLOTS, SLOTS])
        waB = sb("waB", [SLOTS, P])
        wmax = sb("wmax", [P, 2])

        ST = ctx.enter_context(nc.psum_tensor("ST", [P, 2048], F32))
        MX = ctx.enter_context(nc.psum_tensor("MX", [P, 1024], F32))
        O = ctx.enter_context(nc.psum_tensor("O", [P, 1024], F32))

        w_in = sem("w_in"); const_ok = sem("const_ok"); pool_c = sem("pool_c")
        spare = sem("spare")
        x_in = Signal(sem("x_in"), 1, step=16)
        y_out = Signal(sem("y_out"), 1, credit=1, step=16)
        wprep = sem("wprep"); wz = sem("wz"); wz_e = sem("wz_e"); wmx = sem("wmx"); wmx_all = sem("wmx_all")
        wchain = sem("wchain")
        US, NB4 = zip(*[stage_units(l) for l in range(2)])
        names = [[n for n, _ in u] for u in US]
        unit_full = [Signal(sem(f"unit_full{l}"), len(US[l])) for l in range(2)]
        unit_free = {(l, c): Signal(sem(f"unit_free{l}_{c}"), sum(e == c for _, e in US[l]), credit=1)
                     for l in range(2) for c in ("act", "dve")}
        normed = [Signal(sem(f"normed{l}"), NT) for l in range(2)]
        normed2 = Signal(sem("normed2"), NT)
        biased = [Signal(sem(f"biased{l}"), 1) for l in range(2)]
        NW = 2 * 2 * KC
        part1 = Signal(sem("part1"), NW)
        rest1 = Signal(sem("rest1"), NW)
        part2 = Signal(sem("part2"), NW)
        part3 = Signal(sem("part3"), NW)
        proj_ok = Signal(sem("proj_ok"), NW)
        stacked = [Signal(sem(f"stacked{o}"), 12, step=16) for o in range(KC)]
        suffix_ok = Signal(sem("suffix_ok"), 6)
        max_full = Signal(sem("max_full"), RING_TURN)
        max_free = Signal(sem("max_free"), RING_TURN, credit=2)
        negmax_parts = Signal(sem("negmax_parts"), 1)
        negmax_in = Signal(sem("negmax_in"), 1, credit=1, step=16)
        st_full = Signal(sem("st_full"), NEX)
        exp_done = Signal(sem("exp_done"), NEX, credit=2)
        v_set = Signal(sem("v_set"), NT)
        pv_done = Signal(sem("pv_done"), NT, credit=NT)
        o_copied = Signal(sem("o_copied"), 1, credit=1)
        clip_ready = Signal(sem("clip_ready"), 1)
        e_ready = Signal(sem("e_ready"), 1)
        ev_ready = Signal(sem("ev_ready"), 1)
        ln_chain = [Signal(sem(f"ln_chain{l}"), n) for l, n in enumerate((8, 16))]
        root = [Signal(sem(f"root{l}"), l + 1) for l in range(2)]
        rope_chain = Signal(sem("rope_chain"), NW)
        moe_chain = Signal(sem("moe_chain"), MOE_STEPS)
        ff_chain = Signal(sem("ff_chain"), NT // 2)
        m_chain = [Signal(sem(f"m_chain{l}"), n) for l, n in enumerate((4, 5))]
        o_chain = [Signal(sem(f"o_chain{l}"), n) for l, n in enumerate((2, 4))]

        def slot_of(l, name):
            s = names[l].index(name) % 4
            return ST[:, s * 512:(s + 1) * 512]

        def full_count(l, b, name):
            return unit_full[l].sem, unit_full[l].count(b, names[l].index(name) + 1)

        def free_count(l, b, name):
            i = names[l].index(name)
            c = US[l][i][1]
            return unit_free[l, c].sem, unit_free[l, c].count(b, sum(e == c for _, e in US[l][:i + 1]))

        def ring(l, turn, g, i):
            base = 0 if g is None else (NMX + 1)
            return base + i

        block = ctx.enter_context(nc.Block())
        consts = {n: ap for n, ap in a.items()}
        loads = []

        @block.sync
        def _(sp):
            def load(dst, src):
                sp.dma_start(dst, src).then_inc(w_in, 16)
                loads.append(1)
            for n in w:
                load(w[n][:, :, :], a["w_" + n].rearrange("(c p) n -> p c n", p=P))
            load(cos[:, :], a["cos"])
            load(sin[:, :], a["sin"])
            load(w_r[:, :, :], a["w_r"].rearrange("(c p) n -> p c n", p=P))
            load(w_u[:, :, :], a["w_u"].rearrange("(c p) n -> p c n", p=P))
            load(w_v[:, :, :], a["w_v"].rearrange("(c p) n -> p c n", p=P))
            load(bcol[:, :, :], a["bcol"])
            load(lncol[:, :, :], a["lncol"])
            for i, n in enumerate(("bv", "bo", "gamma", "beta")):
                load(brow[:, i, :], a[n].rearrange("(o n) -> o n", o=1).broadcast_to([P, D]))
            load(attrT[:, :], a["attrT"])
            load(waB[:, :], a["waB"])

            for sig in (y_out, negmax_in, unit_free[0, "act"], unit_free[0, "dve"], unit_free[1, "act"], unit_free[1, "dve"]):
                sp.sem_inc(sig.sem, sig.credit * sig.step)
            with sp.Fori(0, B) as b:
                sp.wait_ge(unit_free[1, "dve"].sem, unit_free[1, "dve"].count(b, 0))
                sp.dma_start(x[:, :, :], a["x"][bass.ds(b, 1)].rearrange("o (n p) d -> p (o n) d", p=P)).then_inc(x_in.sem, 16)
                for l in range(2):
                    turn = b * 2 + l
                    for ot in range(KC):
                        sp.wait_ge(part3.sem, part3.count(turn, NW // 2 * (ot + 1)))
                        sp.wait_ge(part2.sem, part2.count(turn, NW // 2 * (ot + 1)))
                        sp.wait_ge(part1.sem, part1.count(turn, NW // 2 * (ot + 1)))
                        for term in range(len(Q_PARTS)):
                            for stack, kind, which in ((QS, 0, Q_PARTS), (KS, 1, K_PARTS)):
                                sp.dma_start(stack[term * DH:(term + 1) * DH, ot * HC * T:(ot + 1) * HC * T],
                                             parts[:, which[term], kind, ot, :]).then_inc(stacked[ot].sem, 16)

                    def send_maxima(g, i):
                        sp.wait_ge(max_free.sem, max_free.count(turn, i + 1))
                        sp.dma_start(
                            QS[KR:KM, bass.ds(g * (GH * T), GH * T)], nmT[0:3 * GH * NT, :],
                        ).then_inc(negmax_in.sem, 16)

                    send_maxima(0, NMX)
                    with sp.Fori(0, NG - 1) as g:
                        send_maxima(g + 1, g * RING + (NMX + 1 + NMX))
                s, v = free_count(1, b, ("wo", NT // 2 - 1))
                sp.wait_ge(s, v)
                sp.dma_start(out[bass.ds(b, 1)].rearrange("o (n p) d -> p (o n) d", p=P), y).then_inc(y_out.sem, 16)
            sp.wait_ge(y_out.sem, y_out.count(B, 0))
        W_IN = 16 * len(loads)

        @block.gpsimd
        def _(pool):
            for t, v in ((ident, 0.0), (identb, 0.0), (negmask, 0.0), (negmaskT, 0.0), (strict, 1.0), (ones, 1.0)):
                pool.memset(t[:, :], v).then_inc(pool_c, 1)
            pool.memset(floor[:, :, :], 0.0).then_inc(pool_c, 1)
            pool.wait_ge(pool_c, 7)
            for t in (ident, identb):
                pool.affine_select(out=t[:, :], in_=t[:, :], compare_op=ALU.not_equal, fill=1.0, base=0,
                                   pattern=[[-1, P]], channel_multiplier=1).then_inc(const_ok, 1)
            pool.affine_select(out=negmask[:, :], in_=negmask[:, :], compare_op=ALU.is_ge, fill=-BIG, base=0,
                               pattern=[[-1, P]], channel_multiplier=1).then_inc(const_ok, 1)
            pool.affine_select(out=negmaskT[:, :], in_=negmaskT[:, :], compare_op=ALU.is_ge, fill=-BIG, base=0,
                               pattern=[[1, P]], channel_multiplier=-1).then_inc(const_ok, 1)
            pool.affine_select(out=strict[:, :], in_=strict[:, :], compare_op=ALU.is_gt, fill=0.0, base=0,
                               pattern=[[-1, P]], channel_multiplier=1).then_inc(const_ok, 1)
            pool.affine_select(out=floor[:, :, :], in_=floor[:, :, :], compare_op=ALU.is_gt, fill=-BIG, base=T - 1,
                               pattern=[[0, GH], [-P, NT]], channel_multiplier=-1).then_inc(const_ok, 1)
            pool.wait_ge(const_ok, 6)
            pool.memset(KS[KR:KM, :], 1.0).then_inc(const_ok, 1)
            pool.wait_ge(const_ok, 7)
            pool.memset(Vst[:, :, :], 0.0).then_inc(const_ok, 1)
            pool.memset(Vaug[:, :], 1.0).then_inc(const_ok, 1)
            pool.wait_ge(wmx, 1)
            pool.partition_all_reduce(wmax[:, 1:2], wmax[:, 0:1], P, bass.bass_isa.ReduceOp.max).then_inc(wmx_all, 1)

            with pool.Fori(0, B) as b:
                for l in range(2):
                    turn = b * 2 + l
                    pool.wait_ge(normed[l].sem, normed[l].count(b, NT))
                    bias = brow[:, 1 if l == 0 else 3, :].unsqueeze(1).broadcast_to([P, NT, D])
                    pool.tensor_tensor(x[:, :, :], x[:, :, :], bias, ALU.add).then_inc(biased[l].sem, 1)
                    for c in range(NW + 1):
                        if c < NW:
                            kind, ot, hf = c % 2, c // 4, c // 2 % 2
                            dst = parts[:, :, kind, ot, hf * 512:(hf + 1) * 512]
                            if c >= 2:
                                pool.wait_ge(part3.sem, part3.count(turn, c - 1))
                            pool.wait_ge(part1.sem, part1.count(turn, c + 1))
                            pool.tensor_tensor(rest[:, c % 2, :], proj[:, c % 2, :], dst[:, 0, :],
                                               ALU.subtract).then_inc(rest1.sem, 1)
                        if c >= 1:
                            d = c - 1
                            kind, ot, hf = d % 2, d // 4, d // 2 % 2
                            dst = parts[:, :, kind, ot, hf * 512:(hf + 1) * 512]
                            pool.wait_ge(part2.sem, part2.count(turn, d + 1))
                            pool.tensor_tensor(dst[:, 2, :], rest[:, d % 2, :], dst[:, 1, :],
                                               ALU.subtract).then_inc(part3.sem, 1)
                    if l == 1:
                        pool.wait_ge(*free_count(1, b, ("v", NT // 2 - 1)))
                        Vt = Vaug[:, :].rearrange("p (n c) -> p n c", n=NT)
                        for n in range(5, -1, -1):
                            prev = Vt[:, 7, :] if n == 5 else suffix[:, n + 1, :]
                            if n < 5:
                                pool.wait_ge(suffix_ok.sem, suffix_ok.count(b, 5 - n))
                            pool.tensor_tensor(suffix[:, n, :], prev, Vt[:, n + 1, :], ALU.add).then_inc(suffix_ok.sem, 1)
                    with pool.Fori(0, NG) as g:
                        G = turn * NG + g
                        gl = b * NG + g
                        for kb in range(NT):
                            pool.wait_ge(pv_done.sem, pv_done.count(G, kb + 1 - NT))
                            if kb == 0:
                                pool.wait_ge(*free_count(l, b, ("v", NT // 2 - 1)))
                            pool.tensor_copy(
                                Vst[:, kb, :].rearrange("p (h c) -> p h c", h=GH)[:, :, 0:VA],
                                Vaug[:, bass.ds(g * (GH * VA) + kb * HEADS * VA, GH * VA)].rearrange("p (h c) -> p h c", h=GH),
                            ).then_inc(v_set.sem, 1)
                            if l == 1 and kb == 4:
                                pool.wait_ge(e_ready.sem, e_ready.count(gl, 1))
                                pool.wait_ge(*free_count(1, b, ("later", 0)))
                                pool.wait_ge(max_free.sem, max_free.count(turn, g * RING + (NMX + 1)))
                                pool.tensor_tensor(
                                    ev.rearrange("p (c v) -> p c v", v=VA),
                                    later_v[:, bass.ds(g * (GH * NT * VA), GH * NT * VA)].rearrange("p (c v) -> p c v", v=VA),
                                    e_all[:, bass.ds(g * (GH * NT), GH * NT)].unsqueeze(2).broadcast_to([P, GH * NT, VA]),
                                    ALU.mult).then_inc(ev_ready.sem, 1)
        CONST_OK = 9

        @block.scalar
        def _(act):
            act.wait_ge(wz, 1)
            act.activation(awb[:, :], ST[:, 0:SLOTS], ACT.Exp, scale=-1.0).then_inc(wz_e, 1)
            act.sem_inc(exp_done.sem, exp_done.credit)
            act.sem_inc(o_copied.sem, o_copied.credit)
            with act.Fori(0, B) as b:
                for l in range(2):
                    turn = b * 2 + l
                    free = unit_free[l, "act"].sem

                    def sqrt(k):
                        act.wait_ge(ln_chain[l].sem, ln_chain[l].count(b, 8 * k + 3))
                        act.activation(std[:, :], veps[:, :], ACT.Sqrt).then_inc(root[l].sem, 1)

                    sqrt(0)
                    for i in range(NT // 2):
                        if i == 0 and l == 0:
                            act.wait_ge(y_out.sem, y_out.count(b, 0))
                        act.wait_ge(*full_count(l, b, ("xT", i)))
                        act.activation(xT[:, :, i * 256:(i + 1) * 256],
                                       slot_of(l, ("xT", i)).rearrange("p (c t) -> p c t", c=KC), ACT.Copy).then_inc(free, 1)
                    if l == 1:
                        sqrt(1)
                    for c in range(NW + 1):
                        if c < NW:
                            kind, ot, hf = c % 2, c // 4, c // 2 % 2
                            dst = parts[:, :, kind, ot, hf * 512:(hf + 1) * 512]
                            act.wait_ge(proj_ok.sem, proj_ok.count(turn, c + 1))
                            act.activation(dst[:, 0, :], proj[:, c % 2, :], ACT.Copy).then_inc(part1.sem, 1)
                        if c >= 1:
                            d = c - 1
                            kind, ot, hf = d % 2, d // 4, d // 2 % 2
                            dst = parts[:, :, kind, ot, hf * 512:(hf + 1) * 512]
                            act.wait_ge(rest1.sem, rest1.count(turn, d + 1))
                            act.activation(dst[:, 1, :], rest[:, d % 2, :], ACT.Copy).then_inc(part2.sem, 1)
                    if l == 0:
                        act.wait_ge(moe_chain.sem, moe_chain.count(b, MOE_EXP_AT))
                        act.activation(r2[:, :, :], r1[:, :, :], ACT.Exp).then_inc(moe_chain.sem, 1)
                        for n in range(NT):
                            act.wait_ge(*full_count(0, b, ("gT", n)))
                            if n >= 2:
                                act.wait_ge(*full_count(0, b, ("ffn", n - 2)))
                            act.activation(ghT[:, n % 2, :, :], slot_of(0, ("gT", n)).rearrange("p (c t) -> p c t", c=FC),
                                           ACT.Copy).then_inc(free, 1)
                    else:
                        for i in range(NT // 2):
                            act.wait_ge(*full_count(1, b, ("x2T", i)))
                            src = slot_of(1, ("x2T", i)).rearrange("p (c t) -> p c t", c=KC)
                            act.activation(xT[:, 0, i * 256:(i + 1) * 256], src[:, 0, :], ACT.Identity,
                                           bias=lncol[:, 1, 0:1], scale=lncol[:, 0, 0:1])
                            act.activation(xT[:, 1, i * 256:(i + 1) * 256], src[:, 1, :], ACT.Identity,
                                           bias=lncol[:, 1, 1:2], scale=lncol[:, 0, 1:2]).then_inc(free, 1)
                    with act.Fori(0, NG) as g:
                        G = turn * NG + g
                        gl = b * NG + g
                        if l == 1:
                            act.wait_ge(clip_ready.sem, clip_ready.count(gl, 1))
                            e_g = e_all[:, bass.ds(g * (GH * NT), GH * NT)]
                            act.activation(e_g, e_g, ACT.Exp, scale=float(SCALE[1])).then_inc(e_ready.sem, 1)
                        for u, (kb, j, n) in enumerate(EXPU):
                            wd = T - kb * P
                            act.wait_ge(st_full.sem, st_full.count(G, u + 1))
                            if j == 0:
                                act.wait_ge(pv_done.sem, pv_done.count(G, kb - 1))
                            tile = ST[:, (u % 2) * 1024:(u % 2 + 1) * 1024]
                            step = wd if n != 2 else 512
                            src = tile[:, 0:n * step].rearrange("p (h q) -> p h q", h=n)[:, :, 0:wd]
                            act.activation(PT[:, kb % 2, j:j + n, 0:wd], src, ACT.Exp,
                                           scale=float(SCALE[l])).then_inc(exp_done.sem, 1)
                        act.wait_ge(pv_done.sem, pv_done.count(G, NT))
                        act.activation(OT, O[:, :], ACT.Copy).then_inc(o_copied.sem, 1)
                    for i in range(NT // 2):
                        act.wait_ge(*full_count(l, b, ("aT", i)))
                        act.activation(attnT[:, :, i * 256:(i + 1) * 256],
                                       slot_of(l, ("aT", i)).rearrange("p (c t) -> p c t", c=KC), ACT.Copy).then_inc(free, 1)

        @block.vector
        def _(dve):
            dve.wait_ge(wz_e, 1)
            wc = [0]

            def wlink(ins):
                wc[0] += 1
                ins.then_inc(wchain, 1)
                dve.wait_ge(wchain, wc[0])

            wlink(dve.tensor_scalar(awb[:, :], awb[:, :], 1.0, None, ALU.add))
            wlink(dve.reciprocal(awb[:, :], awb[:, :]))
            dve.wait_ge(w_in, W_IN)
            dve.tensor_reduce(wmax[:, 0:1], w["f1"][:, :, :], AX.XY, ALU.max, apply_absolute_value=True).then_inc(wmx, 1)
            wlink(dve.tensor_scalar(xT[:, :, 0:D], w["f1"][:, :, :], 0.0, None, ALU.is_lt))
            wlink(dve.tensor_scalar(w["f1"][:, :, :], w["f1"][:, :, :], 0.0, None, ALU.is_gt))
            wlink(dve.tensor_tensor(w["f1"][:, :, :], w["f1"][:, :, :], xT[:, :, 0:D], ALU.subtract))
            dve.wait_ge(wmx_all, 1)
            wlink(dve.tensor_scalar(brow[:, 2, :], brow[:, 2, :], wmax[:, 1:2], None, ALU.mult))
            dve.wait_ge(const_ok, CONST_OK)
            dve.sem_inc(max_free.sem, max_free.credit)

            with dve.Fori(0, B) as b:
                for l in range(2):
                    turn = b * 2 + l
                    free = unit_free[l, "dve"].sem
                    link = Chain(dve, ln_chain[l], b)

                    turn_of_norm = [0]

                    def norm(src, dst, sig):
                        for n in range(NT - 1):
                            dve.bn_stats(stats[:, n, :], src[:, n, :])
                        link(dve.bn_stats(stats[:, NT - 1, :], src[:, NT - 1, :]))
                        wait_apart(dve, link.mark.sem, link.mark.count(b, link.n), spare)
                        for n in range(NT - 1):
                            dve.bn_aggr(mv[:, n, :], stats[:, n, :])
                        link(dve.bn_aggr(mv[:, NT - 1, :], stats[:, NT - 1, :]))
                        link(dve.tensor_scalar(veps[:, :], mv[:, :, 1], EPS, None, ALU.add))
                        dve.wait_ge(root[l].sem, root[l].count(b, turn_of_norm[0] + 1))
                        turn_of_norm[0] += 1
                        link(dve.reciprocal(rstd[:, :], std[:, :]))
                        link(dve.tensor_tensor(std[:, :], rstd[:, :], rstd[:, :], ALU.mult))
                        link(dve.tensor_tensor(std[:, :], std[:, :], veps[:, :], ALU.mult))
                        link(dve.tensor_scalar(std[:, :], std[:, :], -0.5, 1.5, ALU.mult, ALU.add))
                        link(dve.tensor_tensor(rstd[:, :], rstd[:, :], std[:, :], ALU.mult))
                        for n in range(NT):
                            dve.tensor_scalar(dst[:, n, :], src[:, n, :], mv[:, n, 0:1], rstd[:, n:n + 1],
                                              ALU.subtract, ALU.mult).then_inc(sig.sem, 1)

                    if l == 0:
                        dve.wait_ge(x_in.sem, x_in.count(b, 1))
                    else:
                        dve.wait_ge(*free_count(0, b, ("wo", NT // 2 - 1)))
                    norm(x, xn, normed[l])
                    if l == 1:
                        dve.wait_ge(normed[1].sem, normed[1].count(b, NT))
                        dve.wait_ge(*full_count(1, b, ("xT", NT // 2 - 1)))
                        norm(xn, xn, normed2)
                    link.close()

                    rope = Chain(dve, rope_chain, b)
                    for c in range(NW):
                        kind, ot, hf = c % 2, c // 4, c // 2 % 2
                        name = "qk"[kind]
                        tok = slice(hf * 512, (hf + 1) * 512)
                        dve.wait_ge(*full_count(l, b, (name, ot, hf)))
                        if c >= 2:
                            dve.wait_ge(rest1.sem, rest1.count(turn, c - 1))
                        if l == 0:
                            dve.scalar_tensor_tensor(rope_a[:, c % 2, :], slot_of(0, (name, ot, hf)),
                                                     bcol[:, 2 * kind, ot:ot + 1], cos[:, tok],
                                                     ALU.add, ALU.mult).then_inc(free, 1)
                            dve.wait_ge(*full_count(0, b, (name + "s", ot, hf)))
                            dve.scalar_tensor_tensor(rope_b[:, c % 2, :], slot_of(0, (name + "s", ot, hf)),
                                                     bcol[:, 2 * kind + 1, ot:ot + 1], sin[:, tok],
                                                     ALU.add, ALU.mult).then_inc(free, 1)
                            dve.wait_ge(*free_count(0, b, (name + "s", ot, hf)))
                            dve.tensor_tensor(proj[:, c % 2, :], rope_a[:, c % 2, :], rope_b[:, c % 2, :],
                                              ALU.add).then_inc(proj_ok.sem, 1)
                        else:
                            dve.tensor_copy(proj[:, c % 2, :], slot_of(1, (name, ot, hf))).then_inc(free, 1)
                            dve.wait_ge(*free_count(1, b, (name, ot, hf)))
                            dve.sem_inc(proj_ok.sem, 1)
                    for i in range(NT // 2):
                        dve.wait_ge(*full_count(l, b, ("v", i)))
                        dst = Vaug[:, :].rearrange("p (n h c) -> p n h c", n=NT, h=HEADS)[:, 2 * i:2 * i + 2, :, 0:DH]
                        src = slot_of(l, ("v", i)).rearrange("p (n h c) -> p n h c", n=2, h=HEADS)
                        for n in range(2):
                            if l == 0:
                                ins = dve.tensor_tensor(dst[:, n], src[:, n],
                                                        brow[:, 0, :].rearrange("p (h c) -> p h c", h=HEADS), ALU.add)
                            else:
                                ins = dve.tensor_copy(dst[:, n], src[:, n])
                        ins.then_inc(free, 1)

                    if l == 0:
                        moe = Chain(dve, moe_chain, b)
                        moe(dve.memset(pre[:, :, :, 0:SLOTS], 0.0))
                        dve.wait_ge(*full_count(0, b, ("router", 0)))
                        dve.tensor_copy(sc[:, :, :], slot_of(0, ("router", 0))[:, 0:NT * SLOTS]
                                        .rearrange("p (n s) -> p n s", n=NT)).then_inc(free, 1)
                        dve.wait_ge(*free_count(0, b, ("router", 0)))
                        dve.sem_inc(spare, 1)
                        for n in range(NT - 1):
                            dve.max(top8[:, n, :], sc[:, n, :])
                        moe(dve.max(top8[:, NT - 1, :], sc[:, NT - 1, :]))
                        row = lambda ap: ap.unsqueeze(2).broadcast_to([P, NT, SLOTS])
                        best, second = top8[:, :, 0], top8[:, :, 1]
                        moe(dve.tensor_tensor(pre[:, 0, :, SLOTS:], sc[:, :, :], row(second), ALU.is_equal))
                        moe(dve.tensor_tensor(rc[:, 0, :], best, second, ALU.is_gt))
                        moe(dve.tensor_tensor(r2[:, :, :], sc[:, :, :], row(second), ALU.is_gt))
                        moe(dve.tensor_copy(sc_eq := r1[:, :, :], pre[:, 0, :, SLOTS:]))
                        src = 0
                        for s in (1, 2, 4, 8, 16):
                            moe(dve.tensor_tensor(pre[:, 1 - src, :, SLOTS:], pre[:, src, :, SLOTS:],
                                                  pre[:, src, :, SLOTS - s:2 * SLOTS - s], ALU.add))
                            src = 1 - src
                        moe(dve.tensor_scalar(rc[:, 0, :], rc[:, 0, :], -1.0, 2.0, ALU.mult, ALU.add))
                        moe(dve.tensor_tensor(pre[:, src, :, SLOTS:], pre[:, src, :, SLOTS:], row(rc[:, 0, :]), ALU.is_le))
                        moe(dve.tensor_tensor(r1[:, :, :], r1[:, :, :], pre[:, src, :, SLOTS:], ALU.mult))
                        moe(dve.tensor_tensor(pre[:, 1 - src, :, SLOTS:], r1[:, :, :], r2[:, :, :], ALU.add))
                        mask = pre[:, 1 - src, :, SLOTS:]
                        moe(dve.tensor_tensor(r1[:, :, :], sc[:, :, :], row(best), ALU.subtract))
                        assert moe.n == MOE_EXP_AT, moe.n
                        moe.n += 1
                        dve.wait_ge(moe_chain.sem, moe_chain.count(b, moe.n))
                        moe(dve.tensor_reduce(rc[:, 1, :], r2[:, :, :], AX.X, ALU.add))
                        moe(dve.tensor_tensor(r2[:, :, :], r2[:, :, :], mask, ALU.mult))
                        moe(dve.tensor_reduce(rc[:, 2, :], r2[:, :, :], AX.X, ALU.add))
                        moe(dve.scalar_tensor_tensor(rc[:, 3, :], rc[:, 1, :], 1e-8, rc[:, 2, :], ALU.mult, ALU.add))
                        moe(dve.reciprocal(rc[:, 3, :], rc[:, 3, :]))
                        moe(dve.tensor_tensor(r2[:, :, :], r2[:, :, :], row(rc[:, 3, :]), ALU.mult))
                        moe(dve.tensor_tensor(r1[:, :, :], r2[:, :, :], awb[:, :].unsqueeze(1).broadcast_to([P, NT, SLOTS]), ALU.mult))
                        moe(dve.tensor_reduce(rc[:, 4, :], r1[:, :, :], AX.X, ALU.add))
                        moe(dve.tensor_scalar(rc[:, 4, :], rc[:, 4, :], 0.2, 0.9, ALU.mult, ALU.add))
                        moe(dve.tensor_tensor(r2[:, :, :], r2[:, :, :], row(rc[:, 4, :]), ALU.mult))
                        moe.close()
                        for n in range(NT + 2):
                            if n < NT:
                                dve.wait_ge(*full_count(0, b, ("hU", n)))
                                if n >= 2:
                                    dve.wait_ge(*full_count(0, b, ("gT", n - 2)))
                                dve.tensor_tensor(gh[:, n % 2, :].rearrange("p (s r) -> p s r", s=SLOTS),
                                                  slot_of(0, ("hU", n)).rearrange("p (s r) -> p s r", s=SLOTS),
                                                  r2[:, n, :].unsqueeze(2).broadcast_to([P, SLOTS, RANK]),
                                                  ALU.mult).then_inc(free, 1)
                            if n >= 2:
                                m = n - 2
                                dve.wait_ge(*full_count(0, b, ("ffn", m)))
                                if m == 0:
                                    dve.wait_ge(biased[0].sem, biased[0].count(b, 1))
                                dve.tensor_tensor(x[:, m, :], slot_of(0, ("ffn", m))[:, 0:D], x[:, m, :],
                                                  ALU.add).then_inc(free, 1)
                    else:
                        ff = Chain(dve, ff_chain, b)
                        for i in range(NT // 2):
                            dve.wait_ge(*full_count(1, b, ("ffn", i)))
                            if i == 0:
                                dve.wait_ge(biased[1].sem, biased[1].count(b, 1))
                            psum = slot_of(1, ("ffn", i)).rearrange("p (n d) -> p n d", n=2)
                            ff(dve.tensor_tensor(psum, psum, brow[:, 2, :].unsqueeze(1).broadcast_to([P, 2, D]), ALU.mult))
                            dve.tensor_tensor(x[:, 2 * i:2 * i + 2, :], psum, x[:, 2 * i:2 * i + 2, :],
                                              ALU.add).then_inc(free, 1)
                        ff.close()
                        for n in range(NT - 1, -1, -1):
                            dve.wait_ge(*full_count(1, b, ("later", n)))
                            dve.tensor_copy(later_v[:, :].rearrange("p (h n c) -> p h n c", h=HEADS, n=NT)[:, :, n, :],
                                            slot_of(1, ("later", n))[:, 0:HEADS * VA].rearrange("p (h c) -> p h c", h=HEADS)
                                            ).then_inc(free, 1)

                    def maxima(G, g_dst, base):
                        for i, (seg, qb, j, n, wd, diag) in enumerate(MAXU):
                            dve.wait_ge(max_full.sem, max_full.count(turn, base + (i + 1)))
                            bank = MX[:, (i % 2) * 512:(i % 2) * 512 + n * wd]
                            dst = mxa[:, j:j + n, qb:qb + 1] if seg == 0 else mxb[:, j:j + n, qb - 4:qb - 3]
                            dve.tensor_reduce(dst, bank.rearrange("p (h k) -> p h k", h=n), AX.X, ALU.max).then_inc(max_free.sem, 1)
                        dve.wait_ge(max_free.sem, max_free.count(turn, base + NMX))
                        m = Chain(dve, m_chain[l], G // 1 if False else G)
                        m(dve.tensor_tensor(mxa[:, :, 4:8], mxa[:, :, 4:8], mxb[:, :, :], ALU.max))
                        flat = mxa[:, :, :].rearrange("p h n -> p (h n)")
                        if l == 1:
                            m(dve.tensor_tensor(mxa[:, :, :], mxa[:, :, :], floor[:, :, :], ALU.max))
                            dve.tensor_scalar(e_all[:, bass.ds(g_dst * (GH * NT), GH * NT)], flat, -1.0, 0.0,
                                              ALU.mult, ALU.min).then_inc(clip_ready.sem, 1)
                        m(dve.tensor_scalar(nmp[:, 0, :], flat, -1.0, None, ALU.mult))
                        m(dve.scalar_tensor_tensor(mrest[:, :], flat, -1.0, nmp[:, 0, :], ALU.mult, ALU.subtract))
                        m(dve.tensor_copy(nmp[:, 1, :], mrest[:, :]))
                        dve.tensor_tensor(nmp[:, 2, :], mrest[:, :], nmp[:, 1, :], ALU.subtract).then_inc(negmax_parts.sem, 1)
                        m.close()
                        dve.wait_ge(max_full.sem, max_full.count(turn, base + (NMX + 1)))
                        dve.wait_ge(negmax_in.sem, negmax_in.count(turn * NG + g_dst, 0))
                        bank = MX[:, (NMX % 2) * 512:(NMX % 2 + 1) * 512].bitcast(BF16)
                        dve.tensor_copy(nmT[0:3 * GH * NT, :], bank[0:3 * GH * NT, 0:P]).then_inc(max_free.sem, 1)

                    def outputs(g, base, i0):
                        c = Chain(dve, o_chain[l], b * NG + g)
                        for t in range(2):
                            i = i0 + t
                            dve.wait_ge(max_free.sem, max_free.count(turn, base + i))
                            dve.wait_ge(max_full.sem, max_full.count(turn, base + (i + 1)))
                            src = MX[:, (i % 2) * 512:(i % 2 + 1) * 512].rearrange("p (n h c) -> p n h c", n=4, h=GH)
                            if l == 1:
                                if t == 0:
                                    dve.wait_ge(ev_ready.sem, ev_ready.count(b * NG + g, 1))
                                add = ev.rearrange("p (h n c) -> p n h c", h=GH, n=NT)[:, 4 * t:4 * t + 4]
                                for n in range(3):
                                    dve.tensor_tensor(num[:, n], src[:, n, :, 0:VA], add[:, n], ALU.add)
                                c(dve.tensor_tensor(num[:, 3], src[:, 3, :, 0:VA], add[:, 3], ALU.add))
                                src = num
                            c(dve.reciprocal(rec[:, :, :], src[:, :, :, DH]))
                            dst = attn[:, 4 * t:4 * t + 4, bass.ds(g * (GH * DH), GH * DH)]
                            for n in range(4):
                                ins = dve.tensor_tensor(dst[:, n].rearrange("p (h c) -> p h c", h=GH), src[:, n, :, 0:DH],
                                                        rec[:, n, :].unsqueeze(2).broadcast_to([P, GH, DH]), ALU.mult)
                            ins.then_inc(max_free.sem, 1)
                        c.close()

                    maxima(b * NG, 0, 0)
                    with dve.Fori(0, NG - 1) as g:
                        maxima(b * NG + g + 1, g + 1, g * RING + (NMX + 1))
                        outputs(g, g * RING + (NMX + 1), NMX + 1)
                    outputs(NG - 1, (NG - 1) * RING + (NMX + 1), 0)
                    for i in range(NT // 2):
                        dve.wait_ge(*full_count(l, b, ("wo", i)))
                        dst = x if l == 0 else y
                        dve.tensor_tensor(dst[:, 2 * i:2 * i + 2, :], slot_of(l, ("wo", i)).rearrange("p (n d) -> p n d", n=2),
                                          x[:, 2 * i:2 * i + 2, :], ALU.add).then_inc(free, 1)

        @block.tensor
        def _(pe):
            pe.wait_ge(w_in, W_IN)
            pe.matmul(ST[:, 0:SLOTS], waB[:, :], attrT[:, :], start=True, stop=True).then_inc(wz, 1)
            pe.wait_ge(wz_e, 1)
            pe.wait_ge(const_ok, CONST_OK)
            pe.wait_ge(wchain, WCHAIN)
            pe.sem_inc(pv_done.sem, pv_done.credit)

            with pe.Fori(0, B) as b:
                for l in range(2):
                    turn = b * 2 + l
                    full = unit_full[l].sem
                    L = str(l)

                    def unit(name):
                        i = names[l].index(name)
                        if i % NB4[l] >= 4:
                            pe.wait_ge(*free_count(l, b, names[l][i - 4]))
                        return slot_of(l, name)

                    def transposes(kind, src, i):
                        bank = unit((kind, i))
                        for c in range(KC):
                            for n in range(2):
                                mm = pe.transpose(bank[:, (2 * c + n) * P:(2 * c + n + 1) * P],
                                                  src[:, 2 * i + n, c * P:(c + 1) * P], ident[:, :])
                        mm.then_inc(full, 1)

                    def accumulate(dst, pairs):
                        for i, (lhsT, rhs) in enumerate(pairs):
                            mm = pe.matmul(dst, lhsT, rhs, start=(i == 0), stop=(i == len(pairs) - 1))
                        return mm

                    def tokens(weight, n):
                        return [(xT[:, c, n * P:(n + 1) * P], weight[:, c, :]) for c in range(KC)]

                    for i in range(NT // 2):
                        pe.wait_ge(normed[l].sem, normed[l].count(b, 2 * i + 2))
                        transposes("xT", xn, i)
                    kinds = ("q", "qs", "k", "ks") if l == 0 else ("q", "k")
                    for ot in range(KC):
                        for hf in range(2):
                            for kind in kinds:
                                if ot == 0 and kind == "q":
                                    pe.wait_ge(*free_count(l, b, ("xT", 2 * hf + 1)))
                                accumulate(unit((kind, ot, hf)),
                                           [(w[kind + L][:, c, ot * P:(ot + 1) * P], xT[:, c, hf * 512:(hf + 1) * 512])
                                            for c in range(KC)]).then_inc(full, 1)
                    for i in range(NT // 2):
                        bank = unit(("v", i))
                        for n in range(2):
                            mm = accumulate(bank[:, n * D:(n + 1) * D], tokens(w["v" + L], 2 * i + n))
                        mm.then_inc(full, 1)
                    if l == 0:
                        bank = unit(("router", 0))
                        for n in range(NT):
                            mm = accumulate(bank[:, n * SLOTS:(n + 1) * SLOTS], tokens(w_r, n))
                        mm.then_inc(full, 1)
                        for n in range(NT + 2):
                            if n < NT:
                                accumulate(unit(("hU", n)), tokens(w_u, n)).then_inc(full, 1)
                            if 1 <= n <= NT:
                                m = n - 1
                                pe.wait_ge(*free_count(0, b, ("hU", m)))
                                bank = unit(("gT", m))
                                for c in range(FC):
                                    mm = pe.transpose(bank[:, c * P:(c + 1) * P], gh[:, m % 2, c * P:(c + 1) * P], ident[:, :])
                                mm.then_inc(full, 1)
                            if n >= 2:
                                m = n - 2
                                pe.wait_ge(*free_count(0, b, ("gT", m)))
                                accumulate(unit(("ffn", m))[:, 0:D],
                                           [(ghT[:, m % 2, c, :], w_v[:, c, :]) for c in range(FC)]).then_inc(full, 1)
                    else:
                        for i in range(NT // 2):
                            pe.wait_ge(normed2.sem, normed2.count(b, 2 * i + 2))
                            transposes("x2T", xn, i)
                        for i in range(NT // 2):
                            pe.wait_ge(*free_count(1, b, ("x2T", i)))
                            bank = unit(("ffn", i))
                            for n in range(2):
                                mm = accumulate(bank[:, n * D:(n + 1) * D], tokens(w["f1"], 2 * i + n))
                            mm.then_inc(full, 1)
                        Vt = Vaug[:, :].rearrange("p (n c) -> p n c", n=NT)
                        pe.wait_ge(*free_count(1, b, ("v", NT // 2 - 1)))
                        for n in range(NT - 1, -1, -1):
                            bank = unit(("later", n))[:, 0:HEADS * VA]
                            pairs = [(strict[:, :], Vt[:, n, :])]
                            if n == 6:
                                pairs += [(ones[:, :], Vt[:, 7, :])]
                            elif n < 6:
                                pe.wait_ge(suffix_ok.sem, suffix_ok.count(b, 6 - n))
                                pairs += [(ones[:, :], suffix[:, n, :])]
                            accumulate(bank, pairs).then_inc(full, 1)

                    def max_unit(g, base, i):
                        seg, qb, j, n, wd, diag = MAXU[i]
                        pe.wait_ge(max_free.sem, max_free.count(turn, base + (i - 1)))
                        for k in range(n):
                            h = (j + k) * T
                            o = (i % 2) * 512 + k * wd
                            mm = pe.matmul(MX[:, o:o + wd], QS[0:KR, bass.ds(g * (GH * T) + (h + qb * P), P)],
                                           KS[0:KR, bass.ds(g * (GH * T) + (h + seg * 512), wd)], start=True, stop=not diag)
                            if diag:
                                mm = pe.matmul(MX[:, o + wd - P:o + wd], identb[:, :], negmask[:, :], start=False, stop=True)
                        mm.then_inc(max_full.sem, 1)

                    def transpose_maxima(G, base):
                        pe.wait_ge(max_free.sem, max_free.count(turn, base + (NMX - 1)))
                        pe.wait_ge(negmax_parts.sem, negmax_parts.count(G, 1))
                        bank = MX[:, (NMX % 2) * 512:(NMX % 2 + 1) * 512].bitcast(BF16)
                        pe.transpose(bank[0:3 * GH * NT, 0:P], nmp[:, :, :].rearrange("p a c -> p (a c)"),
                                     identb[:, :]).then_inc(max_full.sem, 1)

                    def st_unit(g, G, u):
                        kb, j, n = EXPU[u]
                        wd = T - kb * P
                        pe.wait_ge(exp_done.sem, exp_done.count(G, u - 1))
                        for k in range(n):
                            h = (j + k) * T
                            o = (u % 2) * 1024 + k * (wd if n != 2 else 512)
                            for q0 in range(0, wd, 512):
                                qw = min(512, wd - q0)
                                mm = pe.matmul(ST[:, o + q0:o + q0 + qw], KS[0:KM, bass.ds(g * (GH * T) + (h + kb * P), P)],
                                               QS[0:KM, bass.ds(g * (GH * T) + (h + kb * P + q0), qw)],
                                               start=True, stop=q0 > 0)
                                if q0 == 0:
                                    mm = pe.matmul(ST[:, o:o + P], identb[:, :], negmaskT[:, :], start=False, stop=True)
                        mm.then_inc(st_full.sem, 1)

                    def pv(G, kb):
                        pe.wait_ge(v_set.sem, v_set.count(G, kb + 1))
                        pe.wait_ge(exp_done.sem, exp_done.count(G, max(i for i, e in enumerate(EXPU) if e[0] == kb) + 1))
                        if kb == 0:
                            pe.wait_ge(o_copied.sem, o_copied.count(G, 0))
                        for half in range(2):
                            q0 = max(kb * P, half * 512)
                            q1 = (half + 1) * 512
                            if q0 >= q1:
                                continue
                            for j in range(GH):
                                mm = pe.matmul(O[32 * j:32 * j + 32, q0:q1], Vst[:, kb, 32 * j:32 * j + 32],
                                               PT[:, kb % 2, j, q0 - kb * P:q1 - kb * P],
                                               start=(kb == 0), stop=(kb == 4 * half + 3), tile_position=(0, 32 * j))
                        mm.then_inc(pv_done.sem, 1)

                    def group(g, max_base, out_base, out_i, with_max):
                        G = turn * NG + g
                        pe.wait_ge(negmax_in.sem, negmax_in.count(G, 1))
                        total = sum((T - kb * P) * n for kb, _, n in EXPU)
                        done, mi = 0, 0
                        for u, (kb, j, n) in enumerate(EXPU):
                            st_unit(g, G, u)
                            if j == 0 and kb >= 1:
                                pv(G, kb - 1)
                            done += (T - kb * P) * n
                            if with_max:
                                while mi < min(NMX, NMX * done / (0.85 * total)):
                                    max_unit(g + 1, max_base, mi)
                                    mi += 1
                        if with_max:
                            transpose_maxima(G + 1, max_base)
                        pv(G, NT - 1)
                        pe.wait_ge(o_copied.sem, o_copied.count(G, 1))
                        for t in range(2):
                            i = out_i + t
                            pe.wait_ge(max_free.sem, max_free.count(turn, out_base + (i - 1)))
                            for n in range(4):
                                c0 = (i % 2) * 512 + n * P
                                mm = pe.transpose(MX[:, c0:c0 + P], OT[:, (4 * t + n) * P:(4 * t + n + 1) * P], ident[:, :])
                            mm.then_inc(max_full.sem, 1)

                    for c in ("act", "dve"):
                        s = unit_free[l, c]
                        pe.wait_ge(s.sem, s.count(b, sum(e == c for _, e in US[l][:NB4[l]])))
                    for o in range(KC):
                        pe.wait_ge(stacked[o].sem, stacked[o].count(turn, 12))
                    for i in range(NMX):
                        max_unit(0, 0, i)
                    transpose_maxima(turn * NG, 0)
                    with pe.Fori(0, NG - 1) as g:
                        group(g, g * RING + (NMX + 1), g * RING + (NMX + 1), NMX + 1, True)
                    group(NG - 1, None, (NG - 1) * RING + (NMX + 1), 0, False)

                    pe.wait_ge(max_free.sem, max_free.count(turn, RING_TURN))
                    for i in range(NT // 2 + 1):
                        if i < NT // 2:
                            transposes("aT", attn, i)
                        if i >= 1:
                            m = i - 1
                            pe.wait_ge(*free_count(l, b, ("aT", m)))
                            bank = unit(("wo", m))
                            for n in range(2):
                                t0 = (2 * m + n) * P
                                mm = accumulate(bank[:, n * D:(n + 1) * D],
                                                [(attnT[:, c, t0:t0 + P], w["o" + L][:, c, :]) for c in range(KC)])
                            mm.then_inc(full, 1)


WCHAIN = 6
MOE_EXP_AT = 16
MOE_STEPS = 27


def tables():
    half = DH // 2
    inv = (np.float32(1.0) / np.power(np.float32(10000.0), np.arange(half, dtype=np.float32) / np.float32(half))).astype(np.float32)
    freqs = np.arange(T, dtype=np.float32)[None, :] * inv[:, None]
    cos = np.repeat(np.cos(freqs), 2, axis=0).astype(np.float32)
    sin = np.repeat(np.sin(freqs), 2, axis=0).astype(np.float32)
    sin[0::2] = -sin[0::2]
    return np.repeat(cos, HC, axis=0), np.repeat(sin, HC, axis=0)


def columns(*vectors):
    return np.stack([v.reshape(KC, P).T for v in vectors], axis=1)


def kernel(**inputs):
    import concourse.bacc as _bacc
    from concourse.bass_utils import run_bass_kernel_spmd as _run

    i = {n: np.asarray(v) for n, v in inputs.items()}
    cols = np.arange(D).reshape(KC, HC, DH).transpose(0, 2, 1).ravel()
    swap = cols ^ 1
    cos, sin = tables()
    arrays = {
        "x": i["L0_attn_x"],
        "w_q0": i["L0_attn_Wq"][cols].T, "w_qs0": i["L0_attn_Wq"][swap].T,
        "w_k0": i["L0_attn_Wk"][cols].T, "w_ks0": i["L0_attn_Wk"][swap].T,
        "w_v0": i["L0_attn_Wv"].T, "w_o0": i["L0_attn_Wo"].T,
        "w_q1": i["L1_attn_Wq"][:, cols], "w_k1": i["L1_attn_Wk"][:, cols], "w_v1": i["L1_attn_Wv"], "w_o1": i["L1_attn_Wo"],
        "w_f1": i["L1_ffn_weight"].T,
        "bcol": columns(i["L0_attn_bq"][cols], i["L0_attn_bq"][swap], i["L0_attn_bk"][cols], i["L0_attn_bk"][swap]),
        "lncol": columns(i["L1_ffn_ln_weight"], i["L1_ffn_ln_bias"]),
        "bv": i["L0_attn_bv"], "bo": i["L0_attn_bo"],
        "w_r": i["L0_ffn_Wr"].T,
        "w_u": i["L0_ffn_U"].transpose(1, 0, 2).reshape(D, FF),
        "w_v": i["L0_ffn_V"].reshape(FF, D),
        "attrT": i["L0_ffn_attr"].T, "waB": np.tile(i["L0_ffn_Wa"].T, (1, P)),
        "gamma": i["L1_ffn_gamma"], "beta": i["L1_ffn_beta"],
        "cos": cos, "sin": sin,
    }
    nc = _bacc.Bacc("TRN2", target_bir_lowering=False, num_devices=1)
    feeds, aps = {}, {}
    for n, v in arrays.items():
        v = np.ascontiguousarray(v)
        feeds[f"in_{n}"] = v
        aps[n] = nc.dram_tensor(f"in_{n}", v.shape, mybir.dt.from_np(v.dtype), kind="ExternalInput").ap()
    out = nc.dram_tensor("out", (B, T, D), F32, kind="ExternalOutput").ap()
    build(nc, aps, out)
    r = _run(nc, [feeds], core_ids=[0])
    return r.results[0]["out"]
```

```python
import concourse.bass as bass
from concourse import mybir
from contextlib import ExitStack
import numpy as np

F32 = mybir.dt.float32
BF16 = mybir.dt.bfloat16
ALU = mybir.AluOpType
ACT = mybir.ActivationFunctionType
AX = mybir.AxisListType

P = 128
B, T, D = 4, 1024, 256
HEADS, DH = 16, 16
NT = T // P
KC = D // P
GH = 4
NG = HEADS // GH
SLOTS, RANK = 32, 16
FF = SLOTS * RANK
FC = FF // P
VA = DH + 1
HC = P // DH
EPS = 1e-5
Q_PARTS = (0, 0, 1, 0, 2, 1)
K_PARTS = (0, 1, 0, 2, 0, 1)
KR = len(Q_PARTS) * DH
KM = KR + 3
BIG = 3.0e38
SCALE = (1.0 / np.sqrt(DH), 1.0 / np.sqrt(T))

def max_units():
    out = []
    for qb in range(NT):
        for seg in range(1 if qb < 4 else 2):
            w = 512 if seg == 0 and qb >= 4 else (qb % 4 + 1) * P
            n = min(512 // w, GH)
            if qb == 0:
                n = 2
            out += [(seg, qb, j, n, w, seg == 1 or qb < 4) for j in range(0, GH, n)]
    return out


def exp_units():
    out = []
    for kb in range(NT):
        n = 1 if kb < 4 else (2 if kb < 6 else 4)
        out += [(kb, j, n) for j in range(0, GH, n)]
    return out


MAXU, EXPU = max_units(), exp_units()
NMX, NEX = len(MAXU), len(EXPU)
RING = NMX + 3
RING_TURN = NG * RING
assert RING % 2 == 0 and NEX % 2 == 0 and (NMX + 1) % 2 == 0


def share(i, n):
    return range(NMX * i // n, NMX * (i + 1) // n)


def stage_units(layer):
    u = [(("xT", i), "act") for i in range(NT // 2)]
    u += [((kind, ot, hf), "dve") for ot in range(KC) for hf in range(2) for kind in "qk"]
    u += [(("v", i), "dve") for i in range(NT // 2)]
    if layer == 0:
        u += [(("router", 0), "dve")]
        for n in range(NT + 2):
            if n < NT:
                u += [(("hU", n), "dve")]
            if 1 <= n <= NT:
                u += [(("gT", n - 1), "act")]
            if n >= 2:
                u += [(("ffn", n - 2), "dve")]
    else:
        u += [(("x2T", i), "act") for i in range(NT // 2)]
        u += [(("ffn", i), "dve") for i in range(NT // 2)]
        u += [(("later", n), "dve") for n in range(NT - 1, -1, -1)]
    n_before = len(u)
    for i in range(NT // 2):
        u += [(("aT", i), "act")]
        u += [(("wo", i - 1), "dve")] if i else []
    u += [(("wo", NT // 2 - 1), "dve")]
    return u, n_before


class Signal:

    def __init__(self, sem, per, turns=1, credit=0, step=1):
        self.sem, self.per, self.turns, self.credit, self.step = sem, per, turns, credit, step

    def count(self, when, n):
        past = when.past(self.per * self.turns * self.step)
        return past + (when.turn * self.per + n + self.credit) * self.step


class Moment:

    def __init__(self, eng, seq, turn=0, kept=None):
        self.eng, self.seq, self.turn = eng, seq, turn
        self.kept = {} if kept is None else kept

    def at(self, turn):
        return Moment(self.eng, self.seq, turn, self.kept)

    def past(self, rise):
        if rise not in self.kept:
            self.kept[rise] = self.eng.snap(self.seq * rise)
        return self.kept[rise]


def wait_apart(eng, sem, count, spare):
    eng.wait_ge(sem, count)
    eng.sem_inc(spare, 1)


class Chain:

    def __init__(self, eng, mark, turn):
        self.eng, self.mark, self.turn, self.n = eng, mark, turn, 0

    def __call__(self, instruction):
        self.n += 1
        instruction.then_inc(self.mark.sem, 1)
        self.eng.wait_ge(self.mark.sem, self.mark.count(self.turn, self.n))

    def close(self):
        assert self.n == self.mark.per, (self.n, self.mark.per)


def build(nc, a, out):
    ctx = ExitStack()
    nc.disable_value_cache = True
    with ctx:
        def sb(name, shape, dt=F32):
            return ctx.enter_context(nc.sbuf_tensor(name, shape, dt))

        def sem(name):
            return ctx.enter_context(nc.semaphore(name))

        QS = sb("QS", [P, HEADS * T], BF16)
        KS = sb("KS", [P, HEADS * T], BF16)
        PTb = sb("PTb", [P, 2 * GH * T])
        PT = PTb[:, :].rearrange("p (s h q) -> p s h q", s=2, h=GH)
        rope_a = PTb[:, 0:1024].rearrange("p (s n) -> p s n", s=2)
        rope_b = PTb[:, 1024:2048].rearrange("p (s n) -> p s n", s=2)
        proj = PTb[:, 2048:3072].rearrange("p (s n) -> p s n", s=2)
        rest = PTb[:, 3072:4096].rearrange("p (s n) -> p s n", s=2)
        gh = PTb[:, 4096:5120].rearrange("p (s n) -> p s n", s=2)
        ghT = PTb[:, 5120:6144].rearrange("p (s c n) -> p s c n", s=2, c=FC)
        suffix = PTb[:, 4096:4096 + 6 * HEADS * VA].rearrange("p (n c) -> p n c", n=6)
        xn = PTb[:, 6144:8192].rearrange("p (n d) -> p n d", n=NT)
        RA = sb("RA", [P, 6144])
        parts = RA[:, :].bitcast(BF16).rearrange("p (i k o q) -> p i k o q", i=3, k=2, o=KC)
        OT = RA[:, 0:T]
        attn = RA[:, 1024:3072].rearrange("p (n d) -> p n d", n=NT)
        attnT = RA[:, 3072:5120].rearrange("p (c t) -> p c t", c=KC)
        x = sb("x", [P, NT, D])
        xT = sb("xT", [P, KC, T])
        y = xT[:, :, :].rearrange("p c t -> p (c t)").rearrange("p (n d) -> p n d", n=NT)
        Vaug = sb("Vaug", [P, NT * HEADS * VA])
        later_v = sb("later_v", [P, HEADS * NT * VA])
        ev = RA[:, 5120:5120 + GH * NT * VA]
        e_all = sb("e_all", [P, HEADS * NT])
        num = RA[:, 5700:5700 + 4 * GH * VA].rearrange("p (n h c) -> p n h c", n=4, h=GH)
        rec = sb("rec", [P, 4, GH])
        mxa = sb("mxa", [P, GH, NT])
        mxb = sb("mxb", [P, GH, 4])
        floor = sb("floor", [P, GH, NT])
        mrest = sb("mrest", [P, GH * NT])
        nmp = sb("nmp", [P, 3, GH * NT], BF16)
        nmT = sb("nmT", [P, P], BF16)
        stats = sb("stats", [P, NT, 6])
        mv = sb("mv", [P, NT, 2])
        rstd = sb("rstd", [P, NT])
        veps = sb("veps", [P, NT])
        std = sb("std", [P, NT])
        sc = later_v[:, 0:NT * SLOTS].rearrange("p (n s) -> p n s", n=NT)
        top8 = sb("top8", [P, NT, 8])
        pre = later_v[:, 512:1536].rearrange("p (i n s) -> p i n s", i=2, n=NT)
        r1 = later_v[:, 256:512].rearrange("p (n s) -> p n s", n=NT)
        r2 = sb("r2", [P, NT, SLOTS])
        rc = sb("rc", [P, 6, NT])
        awb = sb("awb", [P, SLOTS])
        ident = sb("ident", [P, P])
        identb = sb("identb", [P, P], BF16)
        negmask = sb("negmask", [P, P], BF16)
        negmaskT = sb("negmaskT", [P, P], BF16)
        strict = sb("strict", [P, P])
        ones = sb("ones", [P, P])
        w = {n: sb("w_" + n, [P, KC, D]) for n in
             ("q0", "k0", "v0", "o0", "q1", "k1", "v1", "o1", "f1")}
        w_r = sb("w_r", [P, KC, SLOTS])
        w_u = sb("w_u", [P, KC, FF])
        w_v = sb("w_v", [P, FC, D])
        cos = sb("cos", [P, T])
        sin = sb("sin", [P, T])
        bcol = sb("bcol", [P, 2, KC])
        lncol = sb("lncol", [P, 2, KC])
        brow = sb("brow", [P, 4, D])
        attrT = sb("attrT", [SLOTS, SLOTS])
        waB = sb("waB", [SLOTS, P])
        wmax = sb("wmax", [P, 2])

        ST = ctx.enter_context(nc.psum_tensor("ST", [P, 2048], F32))
        MX = ctx.enter_context(nc.psum_tensor("MX", [P, 1024], F32))
        O = ctx.enter_context(nc.psum_tensor("O", [P, 1024], F32))

        w_in = sem("w_in"); const_ok = sem("const_ok"); pool_c = sem("pool_c")
        spare = sem("spare")
        x_in = Signal(sem("x_in"), 1, step=16)
        y_out = Signal(sem("y_out"), 1, credit=1, step=16)
        wprep = sem("wprep"); wz = sem("wz"); wz_e = sem("wz_e"); wmx = sem("wmx"); wmx_all = sem("wmx_all")
        wchain = sem("wchain")
        US, NB4 = zip(*[stage_units(l) for l in range(2)])
        names = [[n for n, _ in u] for u in US]
        unit_full = [Signal(sem(f"unit_full{l}"), len(US[l])) for l in range(2)]
        unit_free = {(l, c): Signal(sem(f"unit_free{l}_{c}"), sum(e == c for _, e in US[l]), credit=1)
                     for l in range(2) for c in ("act", "dve")}
        normed = [Signal(sem(f"normed{l}"), NT) for l in range(2)]
        normed2 = Signal(sem("normed2"), NT)
        biased = [Signal(sem(f"biased{l}"), 1) for l in range(2)]
        NW = 2 * 2 * KC
        part1 = Signal(sem("part1"), NW, turns=2)
        rest1 = Signal(sem("rest1"), NW, turns=2)
        part2 = Signal(sem("part2"), NW, turns=2)
        part3 = Signal(sem("part3"), NW, turns=2)
        proj_ok = Signal(sem("proj_ok"), NW, turns=2)
        stacked = [Signal(sem(f"stacked{o}"), 12, turns=2, step=16) for o in range(KC)]
        suffix_ok = Signal(sem("suffix_ok"), 6)
        max_full = Signal(sem("max_full"), RING_TURN, turns=2)
        max_free = Signal(sem("max_free"), RING_TURN, turns=2, credit=2)
        negmax_parts = Signal(sem("negmax_parts"), 1, turns=2 * NG)
        negmax_in = Signal(sem("negmax_in"), 1, turns=2 * NG, credit=1, step=16)
        st_full = Signal(sem("st_full"), NEX, turns=2 * NG)
        exp_done = Signal(sem("exp_done"), NEX, turns=2 * NG, credit=2)
        pv_done = Signal(sem("pv_done"), NT, turns=2 * NG, credit=NT)
        o_copied = Signal(sem("o_copied"), 1, turns=2 * NG, credit=1)
        clip_ready = Signal(sem("clip_ready"), 1, turns=NG)
        e_ready = Signal(sem("e_ready"), 1, turns=NG)
        ev_ready = Signal(sem("ev_ready"), 1, turns=NG)
        ln_chain = [Signal(sem(f"ln_chain{l}"), n) for l, n in enumerate((8, 16))]
        root = [Signal(sem(f"root{l}"), l + 1) for l in range(2)]
        rope_chain = Signal(sem("rope_chain"), NW)
        moe_chain = Signal(sem("moe_chain"), MOE_STEPS)
        ff_chain = Signal(sem("ff_chain"), NT // 2)
        m_chain = [Signal(sem(f"m_chain{l}"), n, turns=NG) for l, n in enumerate((4, 5))]
        o_chain = [Signal(sem(f"o_chain{l}"), n, turns=NG) for l, n in enumerate((2, 4))]

        def slot_of(l, name):
            s = names[l].index(name) % 4
            return ST[:, s * 512:(s + 1) * 512]

        def full_count(l, b, name):
            return unit_full[l].sem, unit_full[l].count(b, names[l].index(name) + 1)

        def free_count(l, b, name):
            i = names[l].index(name)
            c = US[l][i][1]
            return unit_free[l, c].sem, unit_free[l, c].count(b, sum(e == c for _, e in US[l][:i + 1]))

        def ring(l, turn, g, i):
            base = 0 if g is None else (NMX + 1)
            return base + i

        block = ctx.enter_context(nc.Block())
        consts = {n: ap for n, ap in a.items()}
        loads = []

        @block.sync
        def _(sp):
            def load(dst, src):
                sp.dma_start(dst, src).then_inc(w_in, 16)
                loads.append(1)
            for n in w:
                load(w[n][:, :, :], a["w_" + n].rearrange("(c p) n -> p c n", p=P))
            load(cos[:, :], a["cos"])
            load(sin[:, :], a["sin"])
            load(w_r[:, :, :], a["w_r"].rearrange("(c p) n -> p c n", p=P))
            load(w_u[:, :, :], a["w_u"].rearrange("(c p) n -> p c n", p=P))
            load(w_v[:, :, :], a["w_v"].rearrange("(c p) n -> p c n", p=P))
            load(bcol[:, :, :], a["bcol"])
            load(lncol[:, :, :], a["lncol"])
            for i, n in enumerate(("bv", "bo", "gamma", "beta")):
                load(brow[:, i, :], a[n].rearrange("(o n) -> o n", o=1).broadcast_to([P, D]))
            load(attrT[:, :], a["attrT"])
            load(waB[:, :], a["waB"])

            for sig in (y_out, negmax_in, unit_free[0, "act"], unit_free[0, "dve"], unit_free[1, "act"], unit_free[1, "dve"]):
                sp.sem_inc(sig.sem, sig.credit * sig.step)
            with sp.Fori(0, B) as seq:
                b = Moment(sp, seq)
                sp.wait_ge(unit_free[1, "dve"].sem, unit_free[1, "dve"].count(b, 0))
                sp.dma_start(x[:, :, :], a["x"][bass.ds(seq, 1)].rearrange("o (n p) d -> p (o n) d", p=P)).then_inc(x_in.sem, 16)
                for l in range(2):
                    turn = b.at(l)
                    for ot in range(KC):
                        sp.wait_ge(part3.sem, part3.count(turn, NW // 2 * (ot + 1)))
                        sp.wait_ge(part2.sem, part2.count(turn, NW // 2 * (ot + 1)))
                        sp.wait_ge(part1.sem, part1.count(turn, NW // 2 * (ot + 1)))
                        for term in range(len(Q_PARTS)):
                            for stack, kind, which in ((QS, 0, Q_PARTS), (KS, 1, K_PARTS)):
                                sp.dma_start(stack[term * DH:(term + 1) * DH, ot * HC * T:(ot + 1) * HC * T],
                                             parts[:, which[term], kind, ot, :]).then_inc(stacked[ot].sem, 16)

                    def send_maxima(g, i):
                        sp.wait_ge(max_free.sem, max_free.count(turn, i + 1))
                        sp.dma_start(
                            QS[KR:KM, bass.ds(g * (GH * T), GH * T)], nmT[0:3 * GH * NT, :],
                        ).then_inc(negmax_in.sem, 16)

                    send_maxima(0, NMX)
                    for g in range(NG - 1):
                        send_maxima(g + 1, g * RING + (NMX + 1 + NMX))
                s, v = free_count(1, b, ("wo", NT // 2 - 1))
                sp.wait_ge(s, v)
                sp.dma_start(out[bass.ds(seq, 1)].rearrange("o (n p) d -> p (o n) d", p=P), y).then_inc(y_out.sem, 16)
            sp.wait_ge(y_out.sem, 16 * (B + y_out.credit))
        W_IN = 16 * len(loads)

        @block.gpsimd
        def _(pool):
            for t, v in ((ident, 0.0), (identb, 0.0), (negmask, 0.0), (negmaskT, 0.0), (strict, 1.0), (ones, 1.0)):
                pool.memset(t[:, :], v).then_inc(pool_c, 1)
            pool.memset(floor[:, :, :], 0.0).then_inc(pool_c, 1)
            pool.wait_ge(pool_c, 7)
            for t in (ident, identb):
                pool.affine_select(out=t[:, :], in_=t[:, :], compare_op=ALU.not_equal, fill=1.0, base=0,
                                   pattern=[[-1, P]], channel_multiplier=1).then_inc(const_ok, 1)
            pool.affine_select(out=negmask[:, :], in_=negmask[:, :], compare_op=ALU.is_ge, fill=-BIG, base=0,
                               pattern=[[-1, P]], channel_multiplier=1).then_inc(const_ok, 1)
            pool.affine_select(out=negmaskT[:, :], in_=negmaskT[:, :], compare_op=ALU.is_ge, fill=-BIG, base=0,
                               pattern=[[1, P]], channel_multiplier=-1).then_inc(const_ok, 1)
            pool.affine_select(out=strict[:, :], in_=strict[:, :], compare_op=ALU.is_gt, fill=0.0, base=0,
                               pattern=[[-1, P]], channel_multiplier=1).then_inc(const_ok, 1)
            pool.affine_select(out=floor[:, :, :], in_=floor[:, :, :], compare_op=ALU.is_gt, fill=-BIG, base=T - 1,
                               pattern=[[0, GH], [-P, NT]], channel_multiplier=-1).then_inc(const_ok, 1)
            pool.wait_ge(const_ok, 6)
            pool.memset(KS[KR:KM, :], 1.0).then_inc(const_ok, 1)
            pool.wait_ge(const_ok, 7)
            pool.memset(Vaug[:, :], 1.0).then_inc(const_ok, 1)
            pool.wait_ge(wmx, 1)
            pool.partition_all_reduce(wmax[:, 1:2], wmax[:, 0:1], P, bass.bass_isa.ReduceOp.max).then_inc(wmx_all, 1)

            with pool.Fori(0, B) as seq:
                b = Moment(pool, seq)
                for l in range(2):
                    turn = b.at(l)
                    pool.wait_ge(normed[l].sem, normed[l].count(b, NT))
                    bias = brow[:, 1 if l == 0 else 3, :].unsqueeze(1).broadcast_to([P, NT, D])
                    pool.tensor_tensor(x[:, :, :], x[:, :, :], bias, ALU.add).then_inc(biased[l].sem, 1)
                    for c in range(NW + 1):
                        if c < NW:
                            kind, ot, hf = c % 2, c // 4, c // 2 % 2
                            dst = parts[:, :, kind, ot, hf * 512:(hf + 1) * 512]
                            if c >= 2:
                                pool.wait_ge(part3.sem, part3.count(turn, c - 1))
                            pool.wait_ge(part1.sem, part1.count(turn, c + 1))
                            pool.tensor_tensor(rest[:, c % 2, :], proj[:, c % 2, :], dst[:, 0, :],
                                               ALU.subtract).then_inc(rest1.sem, 1)
                        if c >= 1:
                            d = c - 1
                            kind, ot, hf = d % 2, d // 4, d // 2 % 2
                            dst = parts[:, :, kind, ot, hf * 512:(hf + 1) * 512]
                            pool.wait_ge(part2.sem, part2.count(turn, d + 1))
                            pool.tensor_tensor(dst[:, 2, :], rest[:, d % 2, :], dst[:, 1, :],
                                               ALU.subtract).then_inc(part3.sem, 1)
                    if l == 1:
                        pool.wait_ge(*free_count(1, b, ("v", NT // 2 - 1)))
                        Vt = Vaug[:, :].rearrange("p (n c) -> p n c", n=NT)
                        for n in range(5, -1, -1):
                            prev = Vt[:, 7, :] if n == 5 else suffix[:, n + 1, :]
                            if n < 5:
                                pool.wait_ge(suffix_ok.sem, suffix_ok.count(b, 5 - n))
                            pool.tensor_tensor(suffix[:, n, :], prev, Vt[:, n + 1, :], ALU.add).then_inc(suffix_ok.sem, 1)
                    for g in range(NG):
                        gl = b.at(g)
                        if l == 1:
                            pool.wait_ge(e_ready.sem, e_ready.count(gl, 1))
                            pool.wait_ge(*free_count(1, b, ("later", 0)))
                            pool.wait_ge(max_free.sem, max_free.count(turn, g * RING + (NMX + 1)))
                            pool.tensor_tensor(
                                ev.rearrange("p (c v) -> p c v", v=VA),
                                later_v[:, g * GH * NT * VA:(g + 1) * GH * NT * VA].rearrange("p (c v) -> p c v", v=VA),
                                e_all[:, g * GH * NT:(g + 1) * GH * NT].unsqueeze(2).broadcast_to([P, GH * NT, VA]),
                                ALU.mult).then_inc(ev_ready.sem, 1)
        CONST_OK = 8

        @block.scalar
        def _(act):
            act.wait_ge(wz, 1)
            act.activation(awb[:, :], ST[:, 0:SLOTS], ACT.Exp, scale=-1.0).then_inc(wz_e, 1)
            act.sem_inc(exp_done.sem, exp_done.credit)
            act.sem_inc(o_copied.sem, o_copied.credit)
            with act.Fori(0, B) as seq:
                b = Moment(act, seq)
                for l in range(2):
                    turn = b.at(l)
                    free = unit_free[l, "act"].sem

                    def sqrt(k):
                        act.wait_ge(ln_chain[l].sem, ln_chain[l].count(b, 8 * k + 3))
                        act.activation(std[:, :], veps[:, :], ACT.Sqrt).then_inc(root[l].sem, 1)

                    sqrt(0)
                    for i in range(NT // 2):
                        if i == 0 and l == 0:
                            act.wait_ge(y_out.sem, y_out.count(b, 0))
                        act.wait_ge(*full_count(l, b, ("xT", i)))
                        act.activation(xT[:, :, i * 256:(i + 1) * 256],
                                       slot_of(l, ("xT", i)).rearrange("p (c t) -> p c t", c=KC), ACT.Copy).then_inc(free, 1)
                    if l == 1:
                        sqrt(1)
                    for c in range(NW + 1):
                        if c < NW:
                            kind, ot, hf = c % 2, c // 4, c // 2 % 2
                            dst = parts[:, :, kind, ot, hf * 512:(hf + 1) * 512]
                            act.wait_ge(proj_ok.sem, proj_ok.count(turn, c + 1))
                            act.activation(dst[:, 0, :], proj[:, c % 2, :], ACT.Copy).then_inc(part1.sem, 1)
                        if c >= 1:
                            d = c - 1
                            kind, ot, hf = d % 2, d // 4, d // 2 % 2
                            dst = parts[:, :, kind, ot, hf * 512:(hf + 1) * 512]
                            act.wait_ge(rest1.sem, rest1.count(turn, d + 1))
                            act.activation(dst[:, 1, :], rest[:, d % 2, :], ACT.Copy).then_inc(part2.sem, 1)
                    if l == 0:
                        act.wait_ge(moe_chain.sem, moe_chain.count(b, MOE_EXP_AT))
                        act.activation(r2[:, :, :], r1[:, :, :], ACT.Exp).then_inc(moe_chain.sem, 1)
                        for n in range(NT):
                            act.wait_ge(*full_count(0, b, ("gT", n)))
                            if n >= 2:
                                act.wait_ge(*full_count(0, b, ("ffn", n - 2)))
                            act.activation(ghT[:, n % 2, :, :], slot_of(0, ("gT", n)).rearrange("p (c t) -> p c t", c=FC),
                                           ACT.Copy).then_inc(free, 1)
                    else:
                        for i in range(NT // 2):
                            act.wait_ge(*full_count(1, b, ("x2T", i)))
                            src = slot_of(1, ("x2T", i)).rearrange("p (c t) -> p c t", c=KC)
                            act.activation(xT[:, 0, i * 256:(i + 1) * 256], src[:, 0, :], ACT.Identity,
                                           bias=lncol[:, 1, 0:1], scale=lncol[:, 0, 0:1])
                            act.activation(xT[:, 1, i * 256:(i + 1) * 256], src[:, 1, :], ACT.Identity,
                                           bias=lncol[:, 1, 1:2], scale=lncol[:, 0, 1:2]).then_inc(free, 1)
                    for g in range(NG):
                        G, gl = b.at(l * NG + g), b.at(g)
                        if l == 1:
                            act.wait_ge(clip_ready.sem, clip_ready.count(gl, 1))
                            e_g = e_all[:, bass.ds(g * (GH * NT), GH * NT)]
                            act.activation(e_g, e_g, ACT.Exp, scale=float(SCALE[1])).then_inc(e_ready.sem, 1)
                        for u, (kb, j, n) in enumerate(EXPU):
                            wd = T - kb * P
                            act.wait_ge(st_full.sem, st_full.count(G, u + 1))
                            if j == 0:
                                act.wait_ge(pv_done.sem, pv_done.count(G, kb - 1))
                            tile = ST[:, (u % 2) * 1024:(u % 2 + 1) * 1024]
                            step = wd if n != 2 else 512
                            src = tile[:, 0:n * step].rearrange("p (h q) -> p h q", h=n)[:, :, 0:wd]
                            act.activation(PT[:, kb % 2, j:j + n, 0:wd], src, ACT.Exp,
                                           scale=float(SCALE[l])).then_inc(exp_done.sem, 1)
                        act.wait_ge(pv_done.sem, pv_done.count(G, NT))
                        act.activation(OT, O[:, :], ACT.Copy).then_inc(o_copied.sem, 1)
                    for i in range(NT // 2):
                        act.wait_ge(*full_count(l, b, ("aT", i)))
                        act.activation(attnT[:, :, i * 256:(i + 1) * 256],
                                       slot_of(l, ("aT", i)).rearrange("p (c t) -> p c t", c=KC), ACT.Copy).then_inc(free, 1)

        @block.vector
        def _(dve):
            dve.wait_ge(wz_e, 1)
            wc = [0]

            def wlink(ins):
                wc[0] += 1
                ins.then_inc(wchain, 1)
                dve.wait_ge(wchain, wc[0])

            wlink(dve.tensor_scalar(awb[:, :], awb[:, :], 1.0, None, ALU.add))
            wlink(dve.reciprocal(awb[:, :], awb[:, :]))
            wlink(dve.memset(O[:, :], 0.0))
            dve.wait_ge(w_in, W_IN)
            dve.tensor_reduce(wmax[:, 0:1], w["f1"][:, :, :], AX.XY, ALU.max, apply_absolute_value=True).then_inc(wmx, 1)
            wlink(dve.tensor_scalar(xT[:, :, 0:D], w["f1"][:, :, :], 0.0, None, ALU.is_lt))
            wlink(dve.tensor_scalar(w["f1"][:, :, :], w["f1"][:, :, :], 0.0, None, ALU.is_gt))
            wlink(dve.tensor_tensor(w["f1"][:, :, :], w["f1"][:, :, :], xT[:, :, 0:D], ALU.subtract))
            dve.wait_ge(wmx_all, 1)
            wlink(dve.tensor_scalar(brow[:, 2, :], brow[:, 2, :], wmax[:, 1:2], None, ALU.mult))
            dve.wait_ge(const_ok, CONST_OK)
            dve.sem_inc(max_free.sem, max_free.credit)

            with dve.Fori(0, B) as seq:
                b = Moment(dve, seq)
                for l in range(2):
                    turn = b.at(l)
                    free = unit_free[l, "dve"].sem
                    link = Chain(dve, ln_chain[l], b)

                    turn_of_norm = [0]

                    def norm(src, dst, sig):
                        for n in range(NT - 1):
                            dve.bn_stats(stats[:, n, :], src[:, n, :])
                        link(dve.bn_stats(stats[:, NT - 1, :], src[:, NT - 1, :]))
                        wait_apart(dve, link.mark.sem, link.mark.count(b, link.n), spare)
                        for n in range(NT - 1):
                            dve.bn_aggr(mv[:, n, :], stats[:, n, :])
                        link(dve.bn_aggr(mv[:, NT - 1, :], stats[:, NT - 1, :]))
                        link(dve.tensor_scalar(veps[:, :], mv[:, :, 1], EPS, None, ALU.add))
                        dve.wait_ge(root[l].sem, root[l].count(b, turn_of_norm[0] + 1))
                        turn_of_norm[0] += 1
                        link(dve.reciprocal(rstd[:, :], std[:, :]))
                        link(dve.tensor_tensor(std[:, :], rstd[:, :], rstd[:, :], ALU.mult))
                        link(dve.tensor_tensor(std[:, :], std[:, :], veps[:, :], ALU.mult))
                        link(dve.tensor_scalar(std[:, :], std[:, :], -0.5, 1.5, ALU.mult, ALU.add))
                        link(dve.tensor_tensor(rstd[:, :], rstd[:, :], std[:, :], ALU.mult))
                        for n in range(NT):
                            dve.tensor_scalar(dst[:, n, :], src[:, n, :], mv[:, n, 0:1], rstd[:, n:n + 1],
                                              ALU.subtract, ALU.mult).then_inc(sig.sem, 1)

                    if l == 0:
                        dve.wait_ge(x_in.sem, x_in.count(b, 1))
                    else:
                        dve.wait_ge(*free_count(0, b, ("wo", NT // 2 - 1)))
                    norm(x, xn, normed[l])
                    if l == 1:
                        dve.wait_ge(normed[1].sem, normed[1].count(b, NT))
                        dve.wait_ge(*full_count(1, b, ("xT", NT // 2 - 1)))
                        norm(xn, xn, normed2)
                    link.close()

                    rope = Chain(dve, rope_chain, b)
                    for c in range(NW):
                        kind, ot, hf = c % 2, c // 4, c // 2 % 2
                        name = "qk"[kind]
                        tok = slice(hf * 512, (hf + 1) * 512)
                        dve.wait_ge(*full_count(l, b, (name, ot, hf)))
                        if c >= 2:
                            dve.wait_ge(rest1.sem, rest1.count(turn, c - 1))
                        if l == 0:
                            dve.scalar_tensor_tensor(rope_a[:, c % 2, :], slot_of(0, (name, ot, hf)),
                                                     bcol[:, kind, ot:ot + 1], cos[:, tok], ALU.add, ALU.mult)
                            for to, at in ((0, P // 2), (P // 2, 0)):
                                half = slice(at, at + P // 2)
                                ins = dve.scalar_tensor_tensor(rope_b[to:to + P // 2, c % 2, :],
                                                               slot_of(0, (name, ot, hf))[half, :],
                                                               bcol[half, kind, ot:ot + 1], sin[half, tok],
                                                               ALU.add, ALU.mult)
                            ins.then_inc(free, 1)
                            dve.wait_ge(*free_count(0, b, (name, ot, hf)))
                            dve.tensor_tensor(proj[:, c % 2, :], rope_a[:, c % 2, :], rope_b[:, c % 2, :],
                                              ALU.add).then_inc(proj_ok.sem, 1)
                        else:
                            dve.tensor_copy(proj[:, c % 2, :], slot_of(1, (name, ot, hf))).then_inc(free, 1)
                            dve.wait_ge(*free_count(1, b, (name, ot, hf)))
                            dve.sem_inc(proj_ok.sem, 1)
                    for i in range(NT // 2):
                        dve.wait_ge(*full_count(l, b, ("v", i)))
                        dst = Vaug[:, :].rearrange("p (n h c) -> p n h c", n=NT, h=HEADS)[:, 2 * i:2 * i + 2, :, 0:DH]
                        src = slot_of(l, ("v", i)).rearrange("p (n h c) -> p n h c", n=2, h=HEADS)
                        for n in range(2):
                            if l == 0:
                                ins = dve.tensor_tensor(dst[:, n], src[:, n],
                                                        brow[:, 0, :].rearrange("p (h c) -> p h c", h=HEADS), ALU.add)
                            else:
                                ins = dve.tensor_copy(dst[:, n], src[:, n])
                        ins.then_inc(free, 1)

                    def row_maxima(base, units):
                        for i in units:
                            seg, qb, j, n, wd, _ = MAXU[i]
                            dve.wait_ge(max_full.sem, max_full.count(turn, base + (i + 1)))
                            bank = MX[:, (i % 2) * 512:(i % 2) * 512 + n * wd]
                            dst = mxa[:, j:j + n, qb:qb + 1] if seg == 0 else mxb[:, j:j + n, qb - 4:qb - 3]
                            dve.tensor_reduce(dst, bank.rearrange("p (h k) -> p h k", h=n), AX.X, ALU.max).then_inc(max_free.sem, 1)

                    def send_maxima(g_dst, base):
                        dve.wait_ge(max_free.sem, max_free.count(turn, base + NMX))
                        m = Chain(dve, m_chain[l], b.at(g_dst))
                        m(dve.tensor_tensor(mxa[:, :, 4:8], mxa[:, :, 4:8], mxb[:, :, :], ALU.max))
                        flat = mxa[:, :, :].rearrange("p h n -> p (h n)")
                        if l == 1:
                            m(dve.tensor_tensor(mxa[:, :, :], mxa[:, :, :], floor[:, :, :], ALU.max))
                            dve.tensor_scalar(e_all[:, bass.ds(g_dst * (GH * NT), GH * NT)], flat, -1.0, 0.0,
                                              ALU.mult, ALU.min).then_inc(clip_ready.sem, 1)
                        m(dve.tensor_scalar(nmp[:, 0, :], flat, -1.0, None, ALU.mult))
                        m(dve.scalar_tensor_tensor(mrest[:, :], flat, -1.0, nmp[:, 0, :], ALU.mult, ALU.subtract))
                        m(dve.tensor_copy(nmp[:, 1, :], mrest[:, :]))
                        dve.tensor_tensor(nmp[:, 2, :], mrest[:, :], nmp[:, 1, :], ALU.subtract).then_inc(negmax_parts.sem, 1)
                        m.close()
                        dve.wait_ge(max_full.sem, max_full.count(turn, base + (NMX + 1)))
                        dve.wait_ge(negmax_in.sem, negmax_in.count(b.at(l * NG + g_dst), 0))
                        bank = MX[:, (NMX % 2) * 512:(NMX % 2 + 1) * 512].bitcast(BF16)
                        dve.tensor_copy(nmT[0:3 * GH * NT, :], bank[0:3 * GH * NT, 0:P]).then_inc(max_free.sem, 1)

                    if l == 0:
                        moe = Chain(dve, moe_chain, b)
                        moe(dve.memset(pre[:, :, :, 0:SLOTS], 0.0))
                        dve.wait_ge(*full_count(0, b, ("router", 0)))
                        dve.tensor_copy(sc[:, :, :], slot_of(0, ("router", 0))[:, 0:NT * SLOTS]
                                        .rearrange("p (n s) -> p n s", n=NT)).then_inc(free, 1)
                        dve.wait_ge(*free_count(0, b, ("router", 0)))
                        dve.sem_inc(spare, 1)
                        for n in range(NT - 1):
                            dve.max(top8[:, n, :], sc[:, n, :])
                        moe(dve.max(top8[:, NT - 1, :], sc[:, NT - 1, :]))
                        row = lambda ap: ap.unsqueeze(2).broadcast_to([P, NT, SLOTS])
                        best, second = top8[:, :, 0], top8[:, :, 1]
                        moe(dve.tensor_tensor(pre[:, 0, :, SLOTS:], sc[:, :, :], row(second), ALU.is_equal))
                        moe(dve.tensor_tensor(rc[:, 0, :], best, second, ALU.is_gt))
                        moe(dve.tensor_tensor(r2[:, :, :], sc[:, :, :], row(second), ALU.is_gt))
                        moe(dve.tensor_copy(sc_eq := r1[:, :, :], pre[:, 0, :, SLOTS:]))
                        src = 0
                        for s in (1, 2, 4, 8, 16):
                            moe(dve.tensor_tensor(pre[:, 1 - src, :, SLOTS:], pre[:, src, :, SLOTS:],
                                                  pre[:, src, :, SLOTS - s:2 * SLOTS - s], ALU.add))
                            src = 1 - src
                        moe(dve.tensor_scalar(rc[:, 0, :], rc[:, 0, :], -1.0, 2.0, ALU.mult, ALU.add))
                        moe(dve.tensor_tensor(pre[:, src, :, SLOTS:], pre[:, src, :, SLOTS:], row(rc[:, 0, :]), ALU.is_le))
                        moe(dve.tensor_tensor(r1[:, :, :], r1[:, :, :], pre[:, src, :, SLOTS:], ALU.mult))
                        moe(dve.tensor_tensor(pre[:, 1 - src, :, SLOTS:], r1[:, :, :], r2[:, :, :], ALU.add))
                        mask = pre[:, 1 - src, :, SLOTS:]
                        moe(dve.tensor_tensor(r1[:, :, :], sc[:, :, :], row(best), ALU.subtract))
                        assert moe.n == MOE_EXP_AT, moe.n
                        moe.n += 1
                        dve.wait_ge(moe_chain.sem, moe_chain.count(b, moe.n))
                        moe(dve.tensor_reduce(rc[:, 1, :], r2[:, :, :], AX.X, ALU.add))
                        moe(dve.tensor_tensor(r2[:, :, :], r2[:, :, :], mask, ALU.mult))
                        moe(dve.tensor_reduce(rc[:, 2, :], r2[:, :, :], AX.X, ALU.add))
                        moe(dve.scalar_tensor_tensor(rc[:, 3, :], rc[:, 1, :], 1e-8, rc[:, 2, :], ALU.mult, ALU.add))
                        moe(dve.reciprocal(rc[:, 3, :], rc[:, 3, :]))
                        moe(dve.tensor_tensor(r2[:, :, :], r2[:, :, :], row(rc[:, 3, :]), ALU.mult))
                        moe(dve.tensor_tensor(r1[:, :, :], r2[:, :, :], awb[:, :].unsqueeze(1).broadcast_to([P, NT, SLOTS]), ALU.mult))
                        moe(dve.tensor_reduce(rc[:, 4, :], r1[:, :, :], AX.X, ALU.add))
                        moe(dve.tensor_scalar(rc[:, 4, :], rc[:, 4, :], 0.2, 0.9, ALU.mult, ALU.add))
                        moe(dve.tensor_tensor(r2[:, :, :], r2[:, :, :], row(rc[:, 4, :]), ALU.mult))
                        moe.close()
                        for n in range(NT + 2):
                            if n < NT:
                                dve.wait_ge(*full_count(0, b, ("hU", n)))
                                if n >= 2:
                                    dve.wait_ge(*full_count(0, b, ("gT", n - 2)))
                                dve.tensor_tensor(gh[:, n % 2, :].rearrange("p (s r) -> p s r", s=SLOTS),
                                                  slot_of(0, ("hU", n)).rearrange("p (s r) -> p s r", s=SLOTS),
                                                  r2[:, n, :].unsqueeze(2).broadcast_to([P, SLOTS, RANK]),
                                                  ALU.mult).then_inc(free, 1)
                            if n >= 2:
                                m = n - 2
                                dve.wait_ge(*full_count(0, b, ("ffn", m)))
                                if m == 0:
                                    dve.wait_ge(biased[0].sem, biased[0].count(b, 1))
                                dve.tensor_tensor(x[:, m, :], slot_of(0, ("ffn", m))[:, 0:D], x[:, m, :],
                                                  ALU.add).then_inc(free, 1)
                            row_maxima(0, share(n, NT + 2))
                    else:
                        ff = Chain(dve, ff_chain, b)
                        for i in range(NT // 2):
                            dve.wait_ge(*full_count(1, b, ("ffn", i)))
                            if i == 0:
                                dve.wait_ge(biased[1].sem, biased[1].count(b, 1))
                            psum = slot_of(1, ("ffn", i)).rearrange("p (n d) -> p n d", n=2)
                            ff(dve.tensor_tensor(psum, psum, brow[:, 2, :].unsqueeze(1).broadcast_to([P, 2, D]), ALU.mult))
                            dve.tensor_tensor(x[:, 2 * i:2 * i + 2, :], psum, x[:, 2 * i:2 * i + 2, :],
                                              ALU.add).then_inc(free, 1)
                            row_maxima(0, share(i, NT // 2 + NT))
                        ff.close()
                        for n in range(NT - 1, -1, -1):
                            dve.wait_ge(*full_count(1, b, ("later", n)))
                            dve.tensor_copy(later_v[:, :].rearrange("p (h n c) -> p h n c", h=HEADS, n=NT)[:, :, n, :],
                                            slot_of(1, ("later", n))[:, 0:HEADS * VA].rearrange("p (h c) -> p h c", h=HEADS)
                                            ).then_inc(free, 1)
                            row_maxima(0, share(NT // 2 + NT - 1 - n, NT // 2 + NT))

                    def outputs(g, base, i0):
                        c = Chain(dve, o_chain[l], b.at(g))
                        for t in range(2):
                            i = i0 + t
                            dve.wait_ge(max_free.sem, max_free.count(turn, base + i))
                            dve.wait_ge(max_full.sem, max_full.count(turn, base + (i + 1)))
                            src = MX[:, (i % 2) * 512:(i % 2 + 1) * 512].rearrange("p (n h c) -> p n h c", n=4, h=GH)
                            if l == 1:
                                if t == 0:
                                    dve.wait_ge(ev_ready.sem, ev_ready.count(b.at(g), 1))
                                add = ev.rearrange("p (h n c) -> p n h c", h=GH, n=NT)[:, 4 * t:4 * t + 4]
                                for n in range(3):
                                    dve.tensor_tensor(num[:, n], src[:, n, :, 0:VA], add[:, n], ALU.add)
                                c(dve.tensor_tensor(num[:, 3], src[:, 3, :, 0:VA], add[:, 3], ALU.add))
                                src = num
                            c(dve.reciprocal(rec[:, :, :], src[:, :, :, DH]))
                            dst = attn[:, 4 * t:4 * t + 4, bass.ds(g * (GH * DH), GH * DH)]
                            for n in range(4):
                                ins = dve.tensor_tensor(dst[:, n].rearrange("p (h c) -> p h c", h=GH), src[:, n, :, 0:DH],
                                                        rec[:, n, :].unsqueeze(2).broadcast_to([P, GH, DH]), ALU.mult)
                            ins.then_inc(max_free.sem, 1)
                        c.close()

                    send_maxima(0, 0)
                    for g in range(NG - 1):
                        row_maxima(g * RING + (NMX + 1), range(NMX))
                        send_maxima(g + 1, g * RING + (NMX + 1))
                        outputs(g, g * RING + (NMX + 1), NMX + 1)
                    outputs(NG - 1, (NG - 1) * RING + (NMX + 1), 0)
                    for i in range(NT // 2):
                        dve.wait_ge(*full_count(l, b, ("wo", i)))
                        dst = x if l == 0 else y
                        dve.tensor_tensor(dst[:, 2 * i:2 * i + 2, :], slot_of(l, ("wo", i)).rearrange("p (n d) -> p n d", n=2),
                                          x[:, 2 * i:2 * i + 2, :], ALU.add).then_inc(free, 1)

        @block.tensor
        def _(pe):
            pe.wait_ge(w_in, W_IN)
            pe.matmul(ST[:, 0:SLOTS], waB[:, :], attrT[:, :], start=True, stop=True).then_inc(wz, 1)
            pe.wait_ge(wz_e, 1)
            pe.wait_ge(const_ok, CONST_OK)
            pe.wait_ge(wchain, WCHAIN)
            pe.sem_inc(pv_done.sem, pv_done.credit)

            with pe.Fori(0, B) as seq:
                b = Moment(pe, seq)
                for l in range(2):
                    turn = b.at(l)
                    full = unit_full[l].sem
                    L = str(l)

                    def unit(name):
                        i = names[l].index(name)
                        if i % NB4[l] >= 4:
                            pe.wait_ge(*free_count(l, b, names[l][i - 4]))
                        return slot_of(l, name)

                    def transposes(kind, src, i):
                        bank = unit((kind, i))
                        for c in range(KC):
                            for n in range(2):
                                mm = pe.transpose(bank[:, (2 * c + n) * P:(2 * c + n + 1) * P],
                                                  src[:, 2 * i + n, c * P:(c + 1) * P], ident[:, :])
                        mm.then_inc(full, 1)

                    def accumulate(dst, pairs):
                        for i, (lhsT, rhs) in enumerate(pairs):
                            mm = pe.matmul(dst, lhsT, rhs, start=(i == 0), stop=(i == len(pairs) - 1))
                        return mm

                    def tokens(weight, n):
                        return [(xT[:, c, n * P:(n + 1) * P], weight[:, c, :]) for c in range(KC)]

                    def wait_stacks():
                        for o in range(KC):
                            pe.wait_ge(stacked[o].sem, stacked[o].count(turn, 2 * len(Q_PARTS)))

                    def max_unit(g, base, i):
                        seg, qb, j, n, wd, diag = MAXU[i]
                        pe.wait_ge(max_free.sem, max_free.count(turn, base + (i - 1)))
                        for k in range(n):
                            h = (j + k) * T
                            o = (i % 2) * 512 + k * wd
                            mm = pe.matmul(MX[:, o:o + wd], QS[0:KR, bass.ds(g * (GH * T) + (h + qb * P), P)],
                                           KS[0:KR, bass.ds(g * (GH * T) + (h + seg * 512), wd)], start=True, stop=not diag)
                            if diag:
                                mm = pe.matmul(MX[:, o + wd - P:o + wd], identb[:, :], negmask[:, :], start=False, stop=True)
                        mm.then_inc(max_full.sem, 1)

                    for i in range(NT // 2):
                        pe.wait_ge(normed[l].sem, normed[l].count(b, 2 * i + 2))
                        transposes("xT", xn, i)
                    for ot in range(KC):
                        for hf in range(2):
                            for kind in "qk":
                                if ot == 0 and kind == "q":
                                    pe.wait_ge(*free_count(l, b, ("xT", 2 * hf + 1)))
                                accumulate(unit((kind, ot, hf)),
                                           [(w[kind + L][:, c, ot * P:(ot + 1) * P], xT[:, c, hf * 512:(hf + 1) * 512])
                                            for c in range(KC)]).then_inc(full, 1)
                    for i in range(NT // 2):
                        bank = unit(("v", i))
                        for n in range(2):
                            mm = accumulate(bank[:, n * D:(n + 1) * D], tokens(w["v" + L], 2 * i + n))
                        mm.then_inc(full, 1)
                    if l == 0:
                        bank = unit(("router", 0))
                        for n in range(NT):
                            mm = accumulate(bank[:, n * SLOTS:(n + 1) * SLOTS], tokens(w_r, n))
                        mm.then_inc(full, 1)
                        for n in range(NT + 2):
                            if n < NT:
                                accumulate(unit(("hU", n)), tokens(w_u, n)).then_inc(full, 1)
                            if 1 <= n <= NT:
                                m = n - 1
                                pe.wait_ge(*free_count(0, b, ("hU", m)))
                                bank = unit(("gT", m))
                                for c in range(FC):
                                    mm = pe.transpose(bank[:, c * P:(c + 1) * P], gh[:, m % 2, c * P:(c + 1) * P], ident[:, :])
                                mm.then_inc(full, 1)
                            if n >= 2:
                                m = n - 2
                                pe.wait_ge(*free_count(0, b, ("gT", m)))
                                accumulate(unit(("ffn", m))[:, 0:D],
                                           [(ghT[:, m % 2, c, :], w_v[:, c, :]) for c in range(FC)]).then_inc(full, 1)
                            if n == 0:
                                wait_stacks()
                            for i in share(n, NT + 2):
                                max_unit(0, 0, i)
                    else:
                        for i in range(NT // 2):
                            pe.wait_ge(normed2.sem, normed2.count(b, 2 * i + 2))
                            transposes("x2T", xn, i)
                        for i in range(NT // 2):
                            pe.wait_ge(*free_count(1, b, ("x2T", i)))
                            bank = unit(("ffn", i))
                            for n in range(2):
                                mm = accumulate(bank[:, n * D:(n + 1) * D], tokens(w["f1"], 2 * i + n))
                            mm.then_inc(full, 1)
                            if i == 0:
                                wait_stacks()
                            for k in share(i, NT // 2 + NT):
                                max_unit(0, 0, k)
                        Vt = Vaug[:, :].rearrange("p (n c) -> p n c", n=NT)
                        pe.wait_ge(*free_count(1, b, ("v", NT // 2 - 1)))
                        for n in range(NT - 1, -1, -1):
                            bank = unit(("later", n))[:, 0:HEADS * VA]
                            pairs = [(strict[:, :], Vt[:, n, :])]
                            if n == 6:
                                pairs += [(ones[:, :], Vt[:, 7, :])]
                            elif n < 6:
                                pe.wait_ge(suffix_ok.sem, suffix_ok.count(b, 6 - n))
                                pairs += [(ones[:, :], suffix[:, n, :])]
                            accumulate(bank, pairs).then_inc(full, 1)
                            for k in share(NT // 2 + NT - 1 - n, NT // 2 + NT):
                                max_unit(0, 0, k)

                    if l == 0:
                        pe.wait_ge(*free_count(0, b, ("v", NT // 2 - 1)))
                    def transpose_maxima(g, base):
                        pe.wait_ge(max_free.sem, max_free.count(turn, base + (NMX - 1)))
                        pe.wait_ge(negmax_parts.sem, negmax_parts.count(b.at(l * NG + g), 1))
                        bank = MX[:, (NMX % 2) * 512:(NMX % 2 + 1) * 512].bitcast(BF16)
                        pe.transpose(bank[0:3 * GH * NT, 0:P], nmp[:, :, :].rearrange("p a c -> p (a c)"),
                                     identb[:, :]).then_inc(max_full.sem, 1)

                    def st_unit(g, G, u):
                        kb, j, n = EXPU[u]
                        wd = T - kb * P
                        pe.wait_ge(exp_done.sem, exp_done.count(G, u - 1))
                        for k in range(n):
                            h = (j + k) * T
                            o = (u % 2) * 1024 + k * (wd if n != 2 else 512)
                            for q0 in range(0, wd, 512):
                                qw = min(512, wd - q0)
                                mm = pe.matmul(ST[:, o + q0:o + q0 + qw], KS[0:KM, bass.ds(g * (GH * T) + (h + kb * P), P)],
                                               QS[0:KM, bass.ds(g * (GH * T) + (h + kb * P + q0), qw)],
                                               start=True, stop=q0 > 0)
                                if q0 == 0:
                                    mm = pe.matmul(ST[:, o:o + P], identb[:, :], negmaskT[:, :], start=False, stop=True)
                        mm.then_inc(st_full.sem, 1)

                    def pv(g, G, kb):
                        pe.wait_ge(exp_done.sem, exp_done.count(G, max(i for i, e in enumerate(EXPU) if e[0] == kb) + 1))
                        if kb == 0:
                            pe.wait_ge(o_copied.sem, o_copied.count(G, 0))
                        for half in range(2):
                            q0 = max(kb * P, half * 512)
                            q1 = (half + 1) * 512
                            if q0 >= q1:
                                continue
                            for j in range(GH):
                                v0 = (kb * HEADS + g * GH + j) * VA
                                mm = pe.matmul(O[32 * j:32 * j + VA, q0:q1], Vaug[:, v0:v0 + VA],
                                               PT[:, kb % 2, j, q0 - kb * P:q1 - kb * P],
                                               start=(kb == 0), stop=(kb == 4 * half + 3), tile_position=(0, 32 * j))
                        mm.then_inc(pv_done.sem, 1)

                    def group(g, max_base, out_base, out_i, with_max):
                        G = b.at(l * NG + g)
                        pe.wait_ge(negmax_in.sem, negmax_in.count(G, 1))
                        total = sum((T - kb * P) * n for kb, _, n in EXPU)
                        done, mi = 0, 0
                        for u, (kb, j, n) in enumerate(EXPU):
                            st_unit(g, G, u)
                            if j == 0 and kb >= 1:
                                pv(g, G, kb - 1)
                            done += (T - kb * P) * n
                            if with_max:
                                while mi < min(NMX, NMX * done / (0.85 * total)):
                                    max_unit(g + 1, max_base, mi)
                                    mi += 1
                        if with_max:
                            transpose_maxima(g + 1, max_base)
                        pv(g, G, NT - 1)
                        pe.wait_ge(o_copied.sem, o_copied.count(G, 1))
                        for t in range(2):
                            i = out_i + t
                            pe.wait_ge(max_free.sem, max_free.count(turn, out_base + (i - 1)))
                            for n in range(4):
                                c0 = (i % 2) * 512 + n * P
                                mm = pe.transpose(MX[:, c0:c0 + P], OT[:, (4 * t + n) * P:(4 * t + n + 1) * P], ident[:, :])
                            mm.then_inc(max_full.sem, 1)

                    for c in ("act", "dve"):
                        s = unit_free[l, c]
                        pe.wait_ge(s.sem, s.count(b, sum(e == c for _, e in US[l][:NB4[l]])))
                    transpose_maxima(0, 0)
                    for g in range(NG - 1):
                        group(g, g * RING + (NMX + 1), g * RING + (NMX + 1), NMX + 1, True)
                    group(NG - 1, None, (NG - 1) * RING + (NMX + 1), 0, False)

                    pe.wait_ge(max_free.sem, max_free.count(turn, RING_TURN))
                    for i in range(NT // 2 + 1):
                        if i < NT // 2:
                            transposes("aT", attn, i)
                        if i >= 1:
                            m = i - 1
                            pe.wait_ge(*free_count(l, b, ("aT", m)))
                            bank = unit(("wo", m))
                            for n in range(2):
                                t0 = (2 * m + n) * P
                                mm = accumulate(bank[:, n * D:(n + 1) * D],
                                                [(attnT[:, c, t0:t0 + P], w["o" + L][:, c, :]) for c in range(KC)])
                            mm.then_inc(full, 1)


WCHAIN = 7
MOE_EXP_AT = 16
MOE_STEPS = 27


def tables():
    half = DH // 2
    inv = (np.float32(1.0) / np.power(np.float32(10000.0), np.arange(half, dtype=np.float32) / np.float32(half))).astype(np.float32)
    freqs = np.arange(T, dtype=np.float32)[None, :] * inv[:, None]
    cos = np.repeat(np.cos(freqs), HC, axis=0).astype(np.float32)
    sin = np.repeat(np.sin(freqs), HC, axis=0).astype(np.float32)
    return np.concatenate([cos, cos]), np.concatenate([sin, -sin])


def columns(*vectors):
    return np.stack([v.reshape(KC, P).T for v in vectors], axis=1)


def kernel(**inputs):
    import concourse.bacc as _bacc
    from concourse.bass_utils import run_bass_kernel_spmd as _run

    i = {n: np.asarray(v) for n, v in inputs.items()}
    cols = np.arange(D).reshape(KC, HC, DH // 2, 2).transpose(0, 3, 2, 1).ravel()
    cos, sin = tables()
    arrays = {
        "x": i["L0_attn_x"],
        "w_q0": i["L0_attn_Wq"][cols].T, "w_k0": i["L0_attn_Wk"][cols].T,
        "w_v0": i["L0_attn_Wv"].T, "w_o0": i["L0_attn_Wo"].T,
        "w_q1": i["L1_attn_Wq"][:, cols], "w_k1": i["L1_attn_Wk"][:, cols], "w_v1": i["L1_attn_Wv"], "w_o1": i["L1_attn_Wo"],
        "w_f1": i["L1_ffn_weight"].T,
        "bcol": columns(i["L0_attn_bq"][cols], i["L0_attn_bk"][cols]),
        "lncol": columns(i["L1_ffn_ln_weight"], i["L1_ffn_ln_bias"]),
        "bv": i["L0_attn_bv"], "bo": i["L0_attn_bo"],
        "w_r": i["L0_ffn_Wr"].T,
        "w_u": i["L0_ffn_U"].transpose(1, 0, 2).reshape(D, FF),
        "w_v": i["L0_ffn_V"].reshape(FF, D),
        "attrT": i["L0_ffn_attr"].T, "waB": np.tile(i["L0_ffn_Wa"].T, (1, P)),
        "gamma": i["L1_ffn_gamma"], "beta": i["L1_ffn_beta"],
        "cos": cos, "sin": sin,
    }
    nc = _bacc.Bacc("TRN2", target_bir_lowering=False, num_devices=1)
    feeds, aps = {}, {}
    for n, v in arrays.items():
        v = np.ascontiguousarray(v)
        feeds[f"in_{n}"] = v
        aps[n] = nc.dram_tensor(f"in_{n}", v.shape, mybir.dt.from_np(v.dtype), kind="ExternalInput").ap()
    out = nc.dram_tensor("out", (B, T, D), F32, kind="ExternalOutput").ap()
    build(nc, aps, out)
    r = _run(nc, [feeds], core_ids=[0])
    return r.results[0]["out"]
```

```python
import concourse.bass as bass
from concourse import mybir
from contextlib import ExitStack
import numpy as np

F32 = mybir.dt.float32
BF16 = mybir.dt.bfloat16
ALU = mybir.AluOpType
ACT = mybir.ActivationFunctionType
AX = mybir.AxisListType

P = 128
B, T, D = 4, 1024, 256
HEADS, DH = 16, 16
NT = T // P
KC = D // P
GH = 4
NG = HEADS // GH
SLOTS, RANK = 32, 16
FF = SLOTS * RANK
FC = FF // P
VA = DH + 1
HC = P // DH
EPS = 1e-5
Q_PARTS = (0, 0, 1, 0, 2, 1)
K_PARTS = (0, 1, 0, 2, 0, 1)
KR = len(Q_PARTS) * DH
KM = KR + 3
BIG = 3.0e38
SCALE = (1.0 / np.sqrt(DH), 1.0 / np.sqrt(T))

def max_units():
    out = []
    for qb in range(NT):
        for seg in range(1 if qb < 4 else 2):
            w = 512 if seg == 0 and qb >= 4 else (qb % 4 + 1) * P
            n = min(512 // w, GH)
            if qb == 0:
                n = 2
            out += [(seg, qb, j, n, w, seg == 1 or qb < 4) for j in range(0, GH, n)]
    return out


def exp_units():
    out = []
    for kb in range(NT):
        n = 1 if kb < 4 else (2 if kb < 6 else 4)
        out += [(kb, j, n) for j in range(0, GH, n)]
    return out


MAXU, EXPU = max_units(), exp_units()
NMX, NEX = len(MAXU), len(EXPU)
COPY_AT = 2


def unit_cols(kb, n):
    return (T - kb * P) * n


def attention_order():
    st = [("st", g, u) for g in range(NG) for u in range(NEX)]
    pv = [("pv", g, kb, h) for g in range(NG) for kb in range(NT) for h in range(kb // 4, 2)]
    mx = [("max", g, i) for g in range(1, NG) for i in range(NMX)]
    rows = [("rows", g) for g in range(NG)]
    outs = [("out", g, t) for g in range(NG) for t in range(2)]
    last_unit = {kb: u for u, (kb, _, _) in enumerate(EXPU)}
    act_steps = []
    for g in range(NG):
        for u, (kb, j, _) in enumerate(EXPU):
            act_steps.append(("exp", g, u))
            if (kb, j) == (5, 0):
                act_steps.append(("copy", g, 0))
            if g and u == COPY_AT - 1:
                act_steps.append(("copy", g - 1, 1))
    act_steps.append(("copy", NG - 1, 1))
    hop = 100.0
    pe = act = dve = 0.0
    parts_at = {0: 1300.0}
    done = {}
    landed, free, order = {}, [0.0, 0.0], []

    def run_act(act):
        while act_steps:
            kind, g, i = act_steps[0]
            if kind == "exp":
                kb, j, n = EXPU[i]
                need = [("st", g, i)]
                if j == 0 and (g or kb >= 2):
                    need.append(("pv", g, kb - 2, 1) if kb >= 2 else ("pv", g - 1, kb + 6, 1))
                cost = unit_cols(kb, n) * 0.833 + 190
            else:
                need, cost = [("pv", g, 4 * i + 3, i)], 512 * 0.833 + 190
            if not all(n in done for n in need):
                return act
            act = max([act] + [done[n] + hop for n in need]) + cost
            done[act_steps.pop(0)] = act
        return act

    while st or pv or mx or rows or outs:
        act = run_act(act)
        options = []
        if st:
            _, g, u = st[0]
            kb, j, n = EXPU[u]
            before = ("exp", g, u - 2) if u >= 2 else ("exp", g - 1, u - 2 + NEX)
            if g in landed and (before in done or (g == 0 and u < 2)):
                ready = max(landed[g], done.get(before, 0.0) + hop)
                options.append((ready, ST_RANK, st, unit_cols(kb, n) / 2.4 + 60 * n))
        if pv:
            _, g, kb, h = pv[0]
            copied = ("copy", g - 1, h)
            turned = g == 0 or kb < 4 * h + 3 or ("out", g - 1, h) in done
            if turned and ("exp", g, last_unit[kb]) in done and (kb or not g or copied in done):
                q0 = max(kb * P, h * 512)
                ready = max(done["exp", g, last_unit[kb]], done.get(copied, 0.0) if kb == 0 else 0.0) + hop
                options.append((ready, PV_RANK, pv, ((h + 1) * 512 - q0) * 4 / 2.4))
        bank = free[-2] + hop
        if rows and rows[0][1] in parts_at:
            options.append((max(bank, parts_at[rows[0][1]] + hop), 0, rows, 60))
        if outs and ("copy",) + outs[0][1:] in done:
            options.append((max(bank, done[("copy",) + outs[0][1:]] + hop), 1, outs, 850))
        if mx:
            _, g, i = mx[0]
            _, _, j, n, wd, diag = MAXU[i]
            options.append((bank, MX_RANK, mx, n * wd / 2.4 + 60 * n * diag))
        start, _, queue, cost = min(options, key=lambda o: (max(o[0], pe), o[1]))
        pe = max(pe, start) + cost
        step = queue.pop(0)
        done[step] = pe
        order.append(step)
        if queue is mx:
            dve = max(dve, pe + hop) + n * wd / 0.96 + 60
            free.append(dve)
            if i == NMX - 1:
                dve += 1300
                parts_at[g] = dve
        elif queue is rows:
            dve = max(dve, pe + hop) + 250
            free.append(dve)
            landed[step[1]] = dve + 2500
        elif queue is outs:
            dve = max(dve, pe + hop) + 900
            free.append(dve)
    return order


ST_RANK, PV_RANK, MX_RANK = 3, 4, 2
ORDER = attention_order()
USES = [("max", 0, i) for i in range(NMX)] + [s for s in ORDER if s[0] in ("max", "rows", "out")]
PLACE = {use: i for i, use in enumerate(USES)}
RING_TURN = len(PLACE)
assert RING_TURN % 2 == 0 and NEX % 2 == 0


EARLY = 12


def share(i, n, first=0):
    return range(first + (NMX - first) * i // n, first + (NMX - first) * (i + 1) // n)


WITH_FF = 16


def share_ff(i):
    return range(WITH_FF * i // NT, WITH_FF * (i + 1) // NT)


NW = 2 * 2 * KC
LATE = 2


def chunk(c):
    return "qk"[c % 2], c // 4, c // 2 % 2


def stage_units(layer):
    u = [(("xT", i), "act") for i in range(NT // 2)]
    u += [(chunk(c), "dve") for c in range(NW // 2)]
    u += [(("router", 0), "dve")] if layer == 0 else []
    u += [(("v", i), "dve") for i in range(NT // 2)]
    u += [] if layer else [(chunk(c), "dve") for c in range(NW // 2, NW - LATE)]
    if layer == 0:
        for n in range(NT + 2):
            if n < NT:
                u += [(("hU", n), "dve")]
            if 1 <= n <= NT:
                u += [(("gT", n - 1), "act")]
            if n >= 2:
                u += [(("ffn", n - 2), "dve")]
            if n < LATE:
                u += [(chunk(NW - LATE + n), "dve")]
    else:
        u += [(("x2T", i), "act") for i in range(NT // 2)]
        for i in range(NT // 2):
            u += [(("ffn", i), "dve"), (chunk(NW // 2 + i), "dve")]
        u += [(("later", n), "dve") for n in range(NT - 1, -1, -1)]
    n_before = len(u)
    for i in range(NT // 2):
        u += [(("aT", i), "act")]
        u += [(("wo", i - 1), "dve")] if i else []
    u += [(("wo", NT // 2 - 1), "dve")]
    return u, n_before


class Signal:

    def __init__(self, sem, per, turns=1, credit=0, step=1):
        self.sem, self.per, self.turns, self.credit, self.step = sem, per, turns, credit, step

    def count(self, when, n):
        past = when.past(self.per * self.turns * self.step)
        return past + (when.turn * self.per + n + self.credit) * self.step


class Moment:

    def __init__(self, eng, seq, turn=0, kept=None):
        self.eng, self.seq, self.turn = eng, seq, turn
        self.kept = {} if kept is None else kept

    def at(self, turn):
        return Moment(self.eng, self.seq, turn, self.kept)

    def past(self, rise):
        if self.seq is None:
            return 0
        if rise not in self.kept:
            self.kept[rise] = self.eng.snap(self.seq * rise)
        return self.kept[rise]


def wait_apart(eng, sem, count, spare):
    eng.wait_ge(sem, count)
    eng.sem_inc(spare, 1)


class Chain:

    def __init__(self, eng, mark, turn):
        self.eng, self.mark, self.turn, self.n = eng, mark, turn, 0

    def __call__(self, instruction):
        self.n += 1
        instruction.then_inc(self.mark.sem, 1)
        self.eng.wait_ge(self.mark.sem, self.mark.count(self.turn, self.n))

    def close(self):
        assert self.n == self.mark.per, (self.n, self.mark.per)


def build(nc, a, out):
    ctx = ExitStack()
    nc.disable_value_cache = True
    with ctx:
        def sb(name, shape, dt=F32):
            return ctx.enter_context(nc.sbuf_tensor(name, shape, dt))

        def sem(name):
            return ctx.enter_context(nc.semaphore(name))

        QS = sb("QS", [P, HEADS * T], BF16)
        KS = sb("KS", [P, HEADS * T], BF16)
        PTb = sb("PTb", [P, 2 * GH * T])
        PT = PTb[:, :].rearrange("p (s h q) -> p s h q", s=2, h=GH)
        rope_a = PTb[:, 0:1024].rearrange("p (s n) -> p s n", s=2)
        rope_b = PTb[:, 1024:2048].rearrange("p (s n) -> p s n", s=2)
        x2T = PTb[:, 0:2048].rearrange("p (c t) -> p c t", c=KC)
        proj = PTb[:, 2048:3072].rearrange("p (s n) -> p s n", s=2)
        rest = PTb[:, 3072:4096].rearrange("p (s n) -> p s n", s=2)
        gh = PTb[:, 4096:5120].rearrange("p (s n) -> p s n", s=2)
        ghT = PTb[:, 5120:6144].rearrange("p (s c n) -> p s c n", s=2, c=FC)
        suffix = PTb[:, 4096:4096 + 6 * HEADS * VA].rearrange("p (n c) -> p n c", n=6)
        xn = PTb[:, 6144:8192].rearrange("p (n d) -> p n d", n=NT)
        RA = sb("RA", [P, 6144])
        parts = RA[:, :].bitcast(BF16).rearrange("p (i k o q) -> p i k o q", i=3, k=2, o=KC)
        OT = RA[:, 0:T]
        attn = RA[:, 1024:3072].rearrange("p (n d) -> p n d", n=NT)
        y = attn
        attnT = RA[:, 3072:5120].rearrange("p (c t) -> p c t", c=KC)
        x = sb("x", [P, NT, D])
        xT = sb("xT", [P, KC, T])
        x0 = QS[:, 0:GH * T].bitcast(F32).rearrange("p (n d) -> p n d", n=NT)
        xn0 = QS[:, GH * T:2 * GH * T].bitcast(F32).rearrange("p (n d) -> p n d", n=NT)
        assert GH * T * 2 == NT * D * 4
        Vaug = sb("Vaug", [P, NT * HEADS * VA])
        later_v = sb("later_v", [P, HEADS * NT * VA])
        ev = RA[:, 5120:5120 + GH * NT * VA]
        e_all = sb("e_all", [P, HEADS * NT])
        num = RA[:, 5700:5700 + 4 * GH * VA].rearrange("p (n h c) -> p n h c", n=4, h=GH)
        rec = sb("rec", [P, 4, GH])
        mxa = sb("mxa", [P, GH, NT])
        mxb = sb("mxb", [P, GH, 4])
        floor = sb("floor", [P, GH, NT])
        mrest = sb("mrest", [P, GH * NT])
        nmp = sb("nmp", [P, 3, GH * NT], BF16)
        nmT = sb("nmT", [P, P], BF16)
        stats = sb("stats", [P, NT, 6])
        mv = sb("mv", [P, NT, 2])
        rstd = sb("rstd", [P, NT])
        veps = sb("veps", [P, NT])
        std = sb("std", [P, NT])
        sc = later_v[:, 0:NT * SLOTS].rearrange("p (n s) -> p n s", n=NT)
        top8 = sb("top8", [P, NT, 8])
        pre = later_v[:, 512:1536].rearrange("p (i n s) -> p i n s", i=2, n=NT)
        r1 = later_v[:, 256:512].rearrange("p (n s) -> p n s", n=NT)
        r2 = sb("r2", [P, NT, SLOTS])
        rc = sb("rc", [P, 6, NT])
        awb = sb("awb", [P, SLOTS])
        ident = sb("ident", [P, P])
        identb = sb("identb", [P, P], BF16)
        negmask = sb("negmask", [P, P], BF16)
        negmaskT = sb("negmaskT", [P, P], BF16)
        strict = sb("strict", [P, P])
        ones = sb("ones", [P, P])
        w = {n: sb("w_" + n, [P, KC, D]) for n in
             ("q0", "k0", "v0", "o0", "q1", "k1", "v1", "o1", "f1")}
        w_r = sb("w_r", [P, KC, SLOTS])
        w_u = sb("w_u", [P, KC, FF])
        w_v = sb("w_v", [P, FC, D])
        cos = sb("cos", [P, T])
        sin = sb("sin", [P, T])
        bcol = sb("bcol", [P, 2, KC])
        lncol = sb("lncol", [P, 2, KC])
        brow = sb("brow", [P, 4, D])
        attrT = sb("attrT", [SLOTS, SLOTS])
        waB = sb("waB", [SLOTS, P])
        wmax = sb("wmax", [P, 2])

        ST = ctx.enter_context(nc.psum_tensor("ST", [P, 2048], F32))
        MX = ctx.enter_context(nc.psum_tensor("MX", [P, 1024], F32))
        O = ctx.enter_context(nc.psum_tensor("O", [P, 1024], F32))

        w_in = {n: sem("w_in_" + n) for n in ("first", "qk", "rest")}; const_ok = sem("const_ok"); pool_c = sem("pool_c")
        spare = sem("spare")
        x_in = Signal(sem("x_in"), 1, step=16)
        y_out = Signal(sem("y_out"), 2, credit=1, step=16)
        wprep = sem("wprep"); wz = sem("wz"); wz_e = sem("wz_e"); wmx = sem("wmx"); wmx_all = sem("wmx_all")
        wchain = sem("wchain")
        US, NB4 = zip(*[stage_units(l) for l in range(2)])
        names = [[n for n, _ in u] for u in US]
        unit_full = [Signal(sem(f"unit_full{l}"), len(US[l])) for l in range(2)]
        unit_free = {(l, c): Signal(sem(f"unit_free{l}_{c}"), sum(e == c for _, e in US[l]), credit=1)
                     for l in range(2) for c in ("act", "dve")}
        normed = [Signal(sem(f"normed{l}"), NT) for l in range(2)]
        normed2 = Signal(sem("normed2"), NT)
        biased = [Signal(sem(f"biased{l}"), 1) for l in range(2)]
        part1 = Signal(sem("part1"), NW, turns=2)
        rest1 = Signal(sem("rest1"), NW, turns=2)
        part2 = Signal(sem("part2"), NW, turns=2)
        part3 = Signal(sem("part3"), NW, turns=2)
        proj_ok = Signal(sem("proj_ok"), NW, turns=2)
        stacked = [Signal(sem(f"stacked{o}"), 12, turns=2, step=16) for o in range(KC)]
        suffix_ok = Signal(sem("suffix_ok"), 6)
        max_full = Signal(sem("max_full"), RING_TURN, turns=2)
        max_free = Signal(sem("max_free"), RING_TURN, turns=2, credit=2)
        negmax_parts = Signal(sem("negmax_parts"), 1, turns=2 * NG)
        negmax_in = Signal(sem("negmax_in"), 1, turns=2 * NG, credit=1, step=16)
        st_full = Signal(sem("st_full"), NEX, turns=2 * NG)
        exp_done = Signal(sem("exp_done"), NEX, turns=2 * NG, credit=2)
        pv_done = Signal(sem("pv_done"), NT, turns=2 * NG, credit=NT)
        o_copied = Signal(sem("o_copied"), 2, turns=2 * NG, credit=2)
        clip_ready = Signal(sem("clip_ready"), 1, turns=NG)
        e_ready = Signal(sem("e_ready"), 1, turns=NG)
        ev_ready = Signal(sem("ev_ready"), 1, turns=NG)
        ln_chain = [Signal(sem(f"ln_chain{l}"), n) for l, n in enumerate((8, 16))]
        root = [Signal(sem(f"root{l}"), l + 1) for l in range(2)]
        moe_chain = Signal(sem("moe_chain"), MOE_STEPS)
        ff_chain = Signal(sem("ff_chain"), NT // 2)
        m_chain = [Signal(sem(f"m_chain{l}"), n, turns=NG) for l, n in enumerate((4, 5))]
        o_chain = [Signal(sem(f"o_chain{l}"), n, turns=NG) for l, n in enumerate((2, 4))]

        def slot_of(l, name):
            s = names[l].index(name) % 4
            return ST[:, s * 512:(s + 1) * 512]

        def full_count(l, b, name):
            return unit_full[l].sem, unit_full[l].count(b, names[l].index(name) + 1)

        def free_count(l, b, name):
            i = names[l].index(name)
            c = US[l][i][1]
            return unit_free[l, c].sem, unit_free[l, c].count(b, sum(e == c for _, e in US[l][:i + 1]))

        def bank_of(use):
            i = PLACE[use] % 2
            return MX[:, i * 512:(i + 1) * 512]

        block = ctx.enter_context(nc.Block())
        consts = {n: ap for n, ap in a.items()}
        loads = {n: 0 for n in w_in}

        @block.sync
        def _(sp):
            def load(stage, dst, src):
                sp.dma_start(dst, src).then_inc(w_in[stage], 16)
                loads[stage] += 1

            def load_weight(stage, n):
                load(stage, w[n][:, :, :], a["w_" + n].rearrange("(c p) n -> p c n", p=P))

            def load_x(seq):
                sp.dma_start(x0, seq.rearrange("o (n p) d -> p (o n) d", p=P)).then_inc(x_in.sem, 16)

            load("first", attrT[:, :], a["attrT"])
            load("first", waB[:, :], a["waB"])
            load_x(a["x"][0:1])
            load_weight("first", "f1")
            for i, n in enumerate(("bv", "bo", "gamma", "beta")):
                load("first", brow[:, i, :], a[n].rearrange("(o n) -> o n", o=1).broadcast_to([P, D]))
            load("first", lncol[:, :, :], a["lncol"])
            load_weight("qk", "q0")
            load_weight("qk", "k0")
            load("qk", bcol[:, :, :], a["bcol"])
            load("qk", cos[:, :], a["cos"])
            load("qk", sin[:, :], a["sin"])
            load("rest", w_r[:, :, :], a["w_r"].rearrange("(c p) n -> p c n", p=P))
            for n in ("v0", "o0", "q1", "k1", "v1", "o1"):
                load_weight("rest", n)
                if n == "v0":
                    load("rest", w_u[:, :, :], a["w_u"].rearrange("(c p) n -> p c n", p=P))
                    load("rest", w_v[:, :, :], a["w_v"].rearrange("(c p) n -> p c n", p=P))

            for sig in (y_out, negmax_in, unit_free[0, "act"], unit_free[0, "dve"], unit_free[1, "act"], unit_free[1, "dve"]):
                sp.sem_inc(sig.sem, sig.credit * sig.step)
            with sp.Fori(0, B) as seq:
                b = Moment(sp, seq)
                for l in range(2):
                    turn = b.at(l)
                    if l == 0:
                        sp.wait_ge(biased[0].sem, biased[0].count(b, 1))
                    for ot in range(KC):
                        sp.wait_ge(part3.sem, part3.count(turn, NW // 2 * (ot + 1)))
                        sp.wait_ge(part2.sem, part2.count(turn, NW // 2 * (ot + 1)))
                        sp.wait_ge(part1.sem, part1.count(turn, NW // 2 * (ot + 1)))
                        for term in range(len(Q_PARTS)):
                            for stack, kind, which in ((QS, 0, Q_PARTS), (KS, 1, K_PARTS)):
                                sp.dma_start(stack[term * DH:(term + 1) * DH, ot * HC * T:(ot + 1) * HC * T],
                                             parts[:, which[term], kind, ot, :]).then_inc(stacked[ot].sem, 16)

                    for g in range(NG):
                        sp.wait_ge(max_free.sem, max_free.count(turn, PLACE["rows", g] + 1))
                        sp.dma_start(QS[KR:KM, g * GH * T:(g + 1) * GH * T], nmT[0:3 * GH * NT, :]).then_inc(negmax_in.sem, 16)
                        if (l, g) == (1, 1):
                            sp.wait_ge(st_full.sem, st_full.count(b.at(NG), NEX))
                            load_x(a["x"][1:B + 1][bass.ds(seq, 1)])
                for half in range(2):
                    s, v = free_count(1, b, ("wo", NT // 4 * (half + 1) - 1))
                    sp.wait_ge(s, v)
                    sp.dma_start(out[bass.ds(seq, 1), half * (T // 2):(half + 1) * (T // 2)]
                                 .rearrange("o (n p) d -> p (o n) d", p=P),
                                 y[:, half * (NT // 2):(half + 1) * (NT // 2)]).then_inc(y_out.sem, 16)
            sp.wait_ge(y_out.sem, 16 * (2 * B + y_out.credit))
        W_IN = {n: 16 * c for n, c in loads.items()}

        @block.gpsimd
        def _(pool):
            for t, v in ((ident, 0.0), (identb, 0.0), (negmask, 0.0), (negmaskT, 0.0), (strict, 1.0), (ones, 1.0)):
                pool.memset(t[:, :], v).then_inc(pool_c, 1)
            pool.memset(floor[:, :, :], 0.0).then_inc(pool_c, 1)
            pool.wait_ge(pool_c, 7)
            for t in (ident, identb):
                pool.affine_select(out=t[:, :], in_=t[:, :], compare_op=ALU.not_equal, fill=1.0, base=0,
                                   pattern=[[-1, P]], channel_multiplier=1).then_inc(const_ok, 1)
            pool.affine_select(out=negmask[:, :], in_=negmask[:, :], compare_op=ALU.is_ge, fill=-BIG, base=0,
                               pattern=[[-1, P]], channel_multiplier=1).then_inc(const_ok, 1)
            pool.affine_select(out=negmaskT[:, :], in_=negmaskT[:, :], compare_op=ALU.is_ge, fill=-BIG, base=0,
                               pattern=[[1, P]], channel_multiplier=-1).then_inc(const_ok, 1)
            pool.affine_select(out=strict[:, :], in_=strict[:, :], compare_op=ALU.is_gt, fill=0.0, base=0,
                               pattern=[[-1, P]], channel_multiplier=1).then_inc(const_ok, 1)
            pool.affine_select(out=floor[:, :, :], in_=floor[:, :, :], compare_op=ALU.is_gt, fill=-BIG, base=T - 1,
                               pattern=[[0, GH], [-P, NT]], channel_multiplier=-1).then_inc(const_ok, 1)
            pool.wait_ge(const_ok, 6)
            pool.memset(KS[KR:KM, :], 1.0).then_inc(const_ok, 1)
            pool.wait_ge(const_ok, 7)
            pool.memset(Vaug[:, :], 1.0).then_inc(const_ok, 1)
            pool.wait_ge(wmx, 1)
            pool.partition_all_reduce(wmax[:, 1:2], wmax[:, 0:1], P, bass.bass_isa.ReduceOp.max).then_inc(wmx_all, 1)

            with pool.Fori(0, B) as seq:
                b = Moment(pool, seq)
                for l in range(2):
                    turn = b.at(l)
                    pool.wait_ge(normed[l].sem, normed[l].count(b, NT))
                    if l == 0:
                        pool.wait_ge(unit_free[1, "dve"].sem, unit_free[1, "dve"].count(b, 0))
                    bias = brow[:, 1 if l == 0 else 3, :].unsqueeze(1).broadcast_to([P, NT, D])
                    pool.tensor_tensor(x[:, :, :], x0 if l == 0 else x[:, :, :], bias, ALU.add).then_inc(biased[l].sem, 1)
                    def first_rest(c):
                        kind, ot, hf = c % 2, c // 4, c // 2 % 2
                        if c >= 2:
                            pool.wait_ge(part3.sem, part3.count(turn, c - 1))
                        pool.wait_ge(part1.sem, part1.count(turn, c + 1))
                        pool.tensor_tensor(rest[:, c % 2, :], proj[:, c % 2, :], parts[:, 0, kind, ot, hf * 512:(hf + 1) * 512],
                                           ALU.subtract).then_inc(rest1.sem, 1)

                    def third_part(c):
                        kind, ot, hf = c % 2, c // 4, c // 2 % 2
                        dst = parts[:, :, kind, ot, hf * 512:(hf + 1) * 512]
                        pool.wait_ge(part2.sem, part2.count(turn, c + 1))
                        pool.tensor_tensor(dst[:, 2, :], rest[:, c % 2, :], dst[:, 1, :],
                                           ALU.subtract).then_inc(part3.sem, 1)

                    for c in range(NW // 2 + 1):
                        if c < NW // 2:
                            first_rest(c)
                        if c >= 1:
                            third_part(c - 1)
                    for c in range(NW // 2, NW):
                        first_rest(c)
                        third_part(c)
                    if l == 1:
                        pool.wait_ge(*free_count(1, b, ("v", NT // 2 - 1)))
                        Vt = Vaug[:, :].rearrange("p (n c) -> p n c", n=NT)
                        for n in range(5, -1, -1):
                            prev = Vt[:, 7, :] if n == 5 else suffix[:, n + 1, :]
                            if n < 5:
                                pool.wait_ge(suffix_ok.sem, suffix_ok.count(b, 5 - n))
                            pool.tensor_tensor(suffix[:, n, :], prev, Vt[:, n + 1, :], ALU.add).then_inc(suffix_ok.sem, 1)
                    for g in range(NG):
                        gl = b.at(g)
                        if l == 1:
                            pool.wait_ge(e_ready.sem, e_ready.count(gl, 1))
                            pool.wait_ge(*free_count(1, b, ("later", 0)))
                            if g == 0:
                                pool.wait_ge(stacked[1].sem, stacked[1].count(turn, 2 * len(Q_PARTS)))
                            if g:
                                pool.wait_ge(max_free.sem, max_free.count(turn, PLACE["out", g - 1, 1] + 1))
                            pool.tensor_tensor(
                                ev.rearrange("p (c v) -> p c v", v=VA),
                                later_v[:, g * GH * NT * VA:(g + 1) * GH * NT * VA].rearrange("p (c v) -> p c v", v=VA),
                                e_all[:, g * GH * NT:(g + 1) * GH * NT].unsqueeze(2).broadcast_to([P, GH * NT, VA]),
                                ALU.mult).then_inc(ev_ready.sem, 1)
        CONST_OK = 8

        @block.scalar
        def _(act):
            act.wait_ge(wz, 1)
            act.activation(awb[:, :], ST[:, 0:SLOTS], ACT.Exp, scale=-1.0).then_inc(wz_e, 1)
            act.sem_inc(exp_done.sem, exp_done.credit)
            act.sem_inc(o_copied.sem, o_copied.credit)

            def sqrt(l, when, k):
                act.wait_ge(ln_chain[l].sem, ln_chain[l].count(when, 8 * k + 3))
                act.activation(std[:, :], veps[:, :], ACT.Sqrt).then_inc(root[l].sem, 1)

            sqrt(0, Moment(act, None), 0)
            with act.Fori(0, B) as seq:
                b = Moment(act, seq)
                for l in range(2):
                    turn = b.at(l)
                    free = unit_free[l, "act"].sem

                    if l == 1:
                        sqrt(1, b, 0)
                    for i in range(NT // 2):
                        act.wait_ge(*full_count(l, b, ("xT", i)))
                        act.activation(xT[:, :, i * 256:(i + 1) * 256],
                                       slot_of(l, ("xT", i)).rearrange("p (c t) -> p c t", c=KC), ACT.Copy).then_inc(free, 1)

                    def first_part(c):
                        kind, ot, hf = c % 2, c // 4, c // 2 % 2
                        act.wait_ge(proj_ok.sem, proj_ok.count(turn, c + 1))
                        act.activation(parts[:, 0, kind, ot, hf * 512:(hf + 1) * 512], proj[:, c % 2, :],
                                       ACT.Copy).then_inc(part1.sem, 1)

                    def second_part(c):
                        kind, ot, hf = c % 2, c // 4, c // 2 % 2
                        act.wait_ge(rest1.sem, rest1.count(turn, c + 1))
                        act.activation(parts[:, 1, kind, ot, hf * 512:(hf + 1) * 512], rest[:, c % 2, :],
                                       ACT.Copy).then_inc(part2.sem, 1)

                    if l == 0:
                        act.wait_ge(y_out.sem, y_out.count(b, 0))
                    for c in range(NW // 2 + 1):
                        if c < NW // 2:
                            first_part(c)
                        if c >= 1:
                            second_part(c - 1)
                    if l == 1:
                        sqrt(1, b, 1)
                    for c in range(NW // 2, NW - LATE) if l == 0 else ():
                        first_part(c)
                        second_part(c)
                    if l == 0:
                        act.wait_ge(moe_chain.sem, moe_chain.count(b, MOE_EXP_AT))
                        act.activation(r2[:, :, :], r1[:, :, :], ACT.Exp).then_inc(moe_chain.sem, 1)
                        for n in range(NT):
                            if n < LATE:
                                first_part(NW - LATE + n)
                                second_part(NW - LATE + n)
                            act.wait_ge(*full_count(0, b, ("gT", n)))
                            if n >= 2:
                                act.wait_ge(*full_count(0, b, ("ffn", n - 2)))
                            act.activation(ghT[:, n % 2, :, :], slot_of(0, ("gT", n)).rearrange("p (c t) -> p c t", c=FC),
                                           ACT.Copy).then_inc(free, 1)
                    else:
                        for i in range(NT // 2):
                            act.wait_ge(*full_count(1, b, ("x2T", i)))
                            src = slot_of(1, ("x2T", i)).rearrange("p (c t) -> p c t", c=KC)
                            act.activation(x2T[:, 0, i * 256:(i + 1) * 256], src[:, 0, :], ACT.Identity,
                                           bias=lncol[:, 1, 0:1], scale=lncol[:, 0, 0:1])
                            act.activation(x2T[:, 1, i * 256:(i + 1) * 256], src[:, 1, :], ACT.Identity,
                                           bias=lncol[:, 1, 1:2], scale=lncol[:, 0, 1:2]).then_inc(free, 1)
                        for c in range(NW // 2, NW):
                            first_part(c)
                            second_part(c)

                    def copy_rest(g):
                        act.wait_ge(pv_done.sem, pv_done.count(b.at(l * NG + g), NT))
                        act.activation(OT[:, 512:T], O[:, 512:T], ACT.Copy).then_inc(o_copied.sem, 1)

                    for g in range(NG):
                        G, gl = b.at(l * NG + g), b.at(g)
                        if l == 1:
                            act.wait_ge(clip_ready.sem, clip_ready.count(gl, 1))
                            e_g = e_all[:, bass.ds(g * (GH * NT), GH * NT)]
                            act.activation(e_g, e_g, ACT.Exp, scale=float(SCALE[1])).then_inc(e_ready.sem, 1)
                        for u, (kb, j, n) in enumerate(EXPU):
                            wd = T - kb * P
                            act.wait_ge(st_full.sem, st_full.count(G, u + 1))
                            if j == 0:
                                act.wait_ge(pv_done.sem, pv_done.count(G, kb - 1))
                            tile = ST[:, (u % 2) * 1024:(u % 2 + 1) * 1024]
                            step = wd if n != 2 else 512
                            src = tile[:, 0:n * step].rearrange("p (h q) -> p h q", h=n)[:, :, 0:wd]
                            act.activation(PT[:, kb % 2, j:j + n, 0:wd], src, ACT.Exp,
                                           scale=float(SCALE[l])).then_inc(exp_done.sem, 1)
                            if g and u == COPY_AT - 1:
                                copy_rest(g - 1)
                            if (kb, j) == (5, 0):
                                act.wait_ge(pv_done.sem, pv_done.count(G, 4))
                                act.activation(OT[:, 0:512], O[:, 0:512], ACT.Copy).then_inc(o_copied.sem, 1)
                    copy_rest(NG - 1)
                    if l == 1:
                        sqrt(0, b.at(1), 0)
                    for i in range(NT // 2):
                        act.wait_ge(*full_count(l, b, ("aT", i)))
                        act.activation(attnT[:, :, i * 256:(i + 1) * 256],
                                       slot_of(l, ("aT", i)).rearrange("p (c t) -> p c t", c=KC), ACT.Copy).then_inc(free, 1)

        @block.vector
        def _(dve):
            def moments(link, src, first=0):
                for n in range(first, NT - 1):
                    dve.bn_stats(stats[:, n, :], src[:, n, :])
                link(dve.bn_stats(stats[:, NT - 1, :], src[:, NT - 1, :]))
                wait_apart(dve, link.mark.sem, link.mark.count(link.turn, link.n), spare)
                for n in range(NT - 1):
                    dve.bn_aggr(mv[:, n, :], stats[:, n, :])
                link(dve.bn_aggr(mv[:, NT - 1, :], stats[:, NT - 1, :]))
                link(dve.tensor_scalar(veps[:, :], mv[:, :, 1], EPS, None, ALU.add))

            def normalise(link, roots, src, dst, sig):
                dve.wait_ge(*roots)
                link(dve.reciprocal(rstd[:, :], std[:, :]))
                link(dve.tensor_tensor(std[:, :], rstd[:, :], rstd[:, :], ALU.mult))
                link(dve.tensor_tensor(std[:, :], std[:, :], veps[:, :], ALU.mult))
                link(dve.tensor_scalar(std[:, :], std[:, :], -0.5, 1.5, ALU.mult, ALU.add))
                link(dve.tensor_tensor(rstd[:, :], rstd[:, :], std[:, :], ALU.mult))
                for n in range(NT):
                    dve.tensor_scalar(dst[:, n, :], src[:, n, :], mv[:, n, 0:1], rstd[:, n:n + 1],
                                      ALU.subtract, ALU.mult).then_inc(sig.sem, 1)

            def input_moments(when):
                link = Chain(dve, ln_chain[0], when)
                dve.wait_ge(x_in.sem, x_in.count(when, 1))
                moments(link, x0)
                return link

            def normalise_input(link):
                normalise(link, (root[0].sem, root[0].count(link.turn, 1)), x0, xn0, normed[0])
                link.close()

            dve.wait_ge(wz_e, 1)
            wc = [0]

            def wlink(ins):
                wc[0] += 1
                ins.then_inc(wchain, 1)
                dve.wait_ge(wchain, wc[0])

            wlink(dve.tensor_scalar(awb[:, :], awb[:, :], 1.0, None, ALU.add))
            wlink(dve.reciprocal(awb[:, :], awb[:, :]))
            wlink(dve.memset(O[:, :], 0.0))
            scratch = later_v[:, 0:KC * D].rearrange("p (c n) -> p c n", c=KC)
            dve.wait_ge(w_in["first"], W_IN["first"])
            dve.tensor_reduce(wmax[:, 0:1], w["f1"][:, :, :], AX.XY, ALU.max, apply_absolute_value=True).then_inc(wmx, 1)
            wlink(dve.tensor_scalar(scratch, w["f1"][:, :, :], 0.0, None, ALU.is_lt))
            wlink(dve.tensor_scalar(w["f1"][:, :, :], w["f1"][:, :, :], 0.0, None, ALU.is_gt))
            wlink(dve.tensor_tensor(w["f1"][:, :, :], w["f1"][:, :, :], scratch, ALU.subtract))
            normalise_input(input_moments(Moment(dve, None)))
            dve.wait_ge(wmx_all, 1)
            wlink(dve.tensor_scalar(brow[:, 2, :], brow[:, 2, :], wmax[:, 1:2], None, ALU.mult))
            dve.wait_ge(const_ok, CONST_OK)
            dve.sem_inc(max_free.sem, max_free.credit)

            with dve.Fori(0, B) as seq:
                b = Moment(dve, seq)
                for l in range(2):
                    turn = b.at(l)
                    free = unit_free[l, "dve"].sem
                    if l == 0:
                        dve.wait_ge(w_in["qk"], W_IN["qk"])
                    else:
                        dve.wait_ge(*free_count(0, b, ("wo", NT // 2 - 1)))
                        link = Chain(dve, ln_chain[1], b)
                        moments(link, x, NT - 2)
                        normalise(link, (root[1].sem, root[1].count(b, 1)), x, xn, normed[1])

                    def project(c):
                        kind, ot, hf = c % 2, c // 4, c // 2 % 2
                        name = "qk"[kind]
                        tok = slice(hf * 512, (hf + 1) * 512)
                        dve.wait_ge(*full_count(l, b, (name, ot, hf)))
                        if c >= 2:
                            dve.wait_ge(rest1.sem, rest1.count(turn, c - 1))
                        if l == 0:
                            dve.scalar_tensor_tensor(rope_a[:, c % 2, :], slot_of(0, (name, ot, hf)),
                                                     bcol[:, kind, ot:ot + 1], cos[:, tok], ALU.add, ALU.mult)
                            for to, at in ((0, P // 2), (P // 2, 0)):
                                half = slice(at, at + P // 2)
                                ins = dve.scalar_tensor_tensor(rope_b[to:to + P // 2, c % 2, :],
                                                               slot_of(0, (name, ot, hf))[half, :],
                                                               bcol[half, kind, ot:ot + 1], sin[half, tok],
                                                               ALU.add, ALU.mult)
                            ins.then_inc(free, 1)
                            dve.wait_ge(*free_count(0, b, (name, ot, hf)))
                            dve.tensor_tensor(proj[:, c % 2, :], rope_a[:, c % 2, :], rope_b[:, c % 2, :],
                                              ALU.add).then_inc(proj_ok.sem, 1)
                        else:
                            dve.tensor_copy(proj[:, c % 2, :], slot_of(1, (name, ot, hf))).then_inc(free, 1)
                            dve.wait_ge(*free_count(1, b, (name, ot, hf)))
                            dve.sem_inc(proj_ok.sem, 1)
                    for c in range(NW // 2):
                        project(c)
                    if l == 1:
                        dve.wait_ge(normed[1].sem, normed[1].count(b, NT))
                        dve.wait_ge(*full_count(1, b, ("xT", NT // 2 - 1)))
                        moments(link, xn)
                        normalise(link, (root[1].sem, root[1].count(b, 2)), xn, xn, normed2)
                        link.close()
                    if l == 0:
                        dve.wait_ge(*full_count(0, b, ("router", 0)))
                        dve.tensor_copy(sc[:, :, :], slot_of(0, ("router", 0))[:, 0:NT * SLOTS]
                                        .rearrange("p (n s) -> p n s", n=NT)).then_inc(free, 1)
                    for i in range(NT // 2):
                        dve.wait_ge(*full_count(l, b, ("v", i)))
                        dst = Vaug[:, :].rearrange("p (n h c) -> p n h c", n=NT, h=HEADS)[:, 2 * i:2 * i + 2, :, 0:DH]
                        src = slot_of(l, ("v", i)).rearrange("p (n h c) -> p n h c", n=2, h=HEADS)
                        for n in range(2):
                            if l == 0:
                                ins = dve.tensor_tensor(dst[:, n], src[:, n],
                                                        brow[:, 0, :].rearrange("p (h c) -> p h c", h=HEADS), ALU.add)
                            else:
                                ins = dve.tensor_copy(dst[:, n], src[:, n])
                        ins.then_inc(free, 1)

                    def arrived(use):
                        dve.wait_ge(max_full.sem, max_full.count(turn, PLACE[use] + 1))
                        return bank_of(use)

                    def row_maxima(g, i):
                        seg, qb, j, n, wd, _ = MAXU[i]
                        if i == 0 and g:
                            dve.wait_ge(negmax_parts.sem, negmax_parts.count(b.at(l * NG + g - 1), 1))
                        bank = arrived(("max", g, i))[:, 0:n * wd].rearrange("p (h k) -> p h k", h=n)
                        dst = mxa[:, j:j + n, qb:qb + 1] if seg == 0 else mxb[:, j:j + n, qb - 4:qb - 3]
                        dve.tensor_reduce(dst, bank, AX.X, ALU.max).then_inc(max_free.sem, 1)

                    def split_maxima(g):
                        dve.wait_ge(max_free.sem, max_free.count(turn, PLACE["max", g, NMX - 1] + 1))
                        m = Chain(dve, m_chain[l], b.at(g))
                        m(dve.tensor_tensor(mxa[:, :, 4:8], mxa[:, :, 4:8], mxb[:, :, :], ALU.max))
                        flat = mxa[:, :, :].rearrange("p h n -> p (h n)")
                        if l == 1:
                            m(dve.tensor_tensor(mxa[:, :, :], mxa[:, :, :], floor[:, :, :], ALU.max))
                            dve.tensor_scalar(e_all[:, g * GH * NT:(g + 1) * GH * NT], flat, -1.0, 0.0,
                                              ALU.mult, ALU.min).then_inc(clip_ready.sem, 1)
                        m(dve.tensor_scalar(nmp[:, 0, :], flat, -1.0, None, ALU.mult))
                        m(dve.scalar_tensor_tensor(mrest[:, :], flat, -1.0, nmp[:, 0, :], ALU.mult, ALU.subtract))
                        m(dve.tensor_copy(nmp[:, 1, :], mrest[:, :]))
                        dve.tensor_tensor(nmp[:, 2, :], mrest[:, :], nmp[:, 1, :], ALU.subtract).then_inc(negmax_parts.sem, 1)
                        m.close()

                    def send_maxima(g):
                        bank = arrived(("rows", g)).bitcast(BF16)
                        dve.wait_ge(negmax_in.sem, negmax_in.count(b.at(l * NG + g), 0))
                        dve.tensor_copy(nmT[0:3 * GH * NT, :], bank[0:3 * GH * NT, 0:P]).then_inc(max_free.sem, 1)

                    o_links = {}

                    def outputs(g, t):
                        c = o_links.setdefault(g, Chain(dve, o_chain[l], b.at(g)))
                        last = ("out", g, 0) if t else ("out", g - 1, 1)
                        if g or t:
                            dve.wait_ge(max_free.sem, max_free.count(turn, PLACE[last] + 1))
                        src = arrived(("out", g, t)).rearrange("p (n h c) -> p n h c", n=4, h=GH)
                        if l == 1:
                            if t == 0:
                                dve.wait_ge(ev_ready.sem, ev_ready.count(b.at(g), 1))
                            add = ev.rearrange("p (h n c) -> p n h c", h=GH, n=NT)[:, 4 * t:4 * t + 4]
                            for n in range(3):
                                dve.tensor_tensor(num[:, n], src[:, n, :, 0:VA], add[:, n], ALU.add)
                            c(dve.tensor_tensor(num[:, 3], src[:, 3, :, 0:VA], add[:, 3], ALU.add))
                            src = num
                        c(dve.reciprocal(rec[:, :, :], src[:, :, :, DH]))
                        dst = attn[:, 4 * t:4 * t + 4, g * GH * DH:(g + 1) * GH * DH]
                        for n in range(4):
                            ins = dve.tensor_tensor(dst[:, n].rearrange("p (h c) -> p h c", h=GH), src[:, n, :, 0:DH],
                                                    rec[:, n, :].unsqueeze(2).broadcast_to([P, GH, DH]), ALU.mult)
                        ins.then_inc(max_free.sem, 1)
                        if t:
                            c.close()

                    def ring_use(use):
                        if use[0] == "max":
                            row_maxima(use[1], use[2])
                            if use[2] == NMX - 1:
                                split_maxima(use[1])
                        elif use[0] == "rows":
                            send_maxima(use[1])
                        else:
                            outputs(use[1], use[2])

                    if l == 0:
                        moe = Chain(dve, moe_chain, b)

                        def early(i):
                            for k in range(EARLY * i // 5, EARLY * (i + 1) // 5):
                                row_maxima(0, k)

                        moe(dve.memset(pre[:, :, :, 0:SLOTS], 0.0))
                        dve.wait_ge(*free_count(0, b, ("router", 0)))
                        dve.sem_inc(spare, 1)
                        for n in range(NT - 1):
                            dve.max(top8[:, n, :], sc[:, n, :])
                        moe(dve.max(top8[:, NT - 1, :], sc[:, NT - 1, :]))
                        row = lambda ap: ap.unsqueeze(2).broadcast_to([P, NT, SLOTS])
                        best, second = top8[:, :, 0], top8[:, :, 1]
                        moe(dve.tensor_tensor(pre[:, 0, :, SLOTS:], sc[:, :, :], row(second), ALU.is_equal))
                        moe(dve.tensor_tensor(rc[:, 0, :], best, second, ALU.is_gt))
                        moe(dve.tensor_tensor(r2[:, :, :], sc[:, :, :], row(second), ALU.is_gt))
                        project(NW - LATE - 2)
                        project(NW - LATE - 1)
                        moe(dve.tensor_copy(sc_eq := r1[:, :, :], pre[:, 0, :, SLOTS:]))
                        src = 0
                        for s in (1, 2, 4, 8, 16):
                            moe(dve.tensor_tensor(pre[:, 1 - src, :, SLOTS:], pre[:, src, :, SLOTS:],
                                                  pre[:, src, :, SLOTS - s:2 * SLOTS - s], ALU.add))
                            src = 1 - src
                        early(0)
                        moe(dve.tensor_scalar(rc[:, 0, :], rc[:, 0, :], -1.0, 2.0, ALU.mult, ALU.add))
                        moe(dve.tensor_tensor(pre[:, src, :, SLOTS:], pre[:, src, :, SLOTS:], row(rc[:, 0, :]), ALU.is_le))
                        moe(dve.tensor_tensor(r1[:, :, :], r1[:, :, :], pre[:, src, :, SLOTS:], ALU.mult))
                        moe(dve.tensor_tensor(pre[:, 1 - src, :, SLOTS:], r1[:, :, :], r2[:, :, :], ALU.add))
                        mask = pre[:, 1 - src, :, SLOTS:]
                        early(1)
                        moe(dve.tensor_tensor(r1[:, :, :], sc[:, :, :], row(best), ALU.subtract))
                        assert moe.n == MOE_EXP_AT, moe.n
                        early(2)
                        moe.n += 1
                        dve.wait_ge(moe_chain.sem, moe_chain.count(b, moe.n))
                        moe(dve.tensor_reduce(rc[:, 1, :], r2[:, :, :], AX.X, ALU.add))
                        moe(dve.tensor_tensor(r2[:, :, :], r2[:, :, :], mask, ALU.mult))
                        moe(dve.tensor_reduce(rc[:, 2, :], r2[:, :, :], AX.X, ALU.add))
                        moe(dve.scalar_tensor_tensor(rc[:, 3, :], rc[:, 1, :], 1e-8, rc[:, 2, :], ALU.mult, ALU.add))
                        early(3)
                        moe(dve.reciprocal(rc[:, 3, :], rc[:, 3, :]))
                        moe(dve.tensor_tensor(r2[:, :, :], r2[:, :, :], row(rc[:, 3, :]), ALU.mult))
                        moe(dve.tensor_tensor(r1[:, :, :], r2[:, :, :], awb[:, :].unsqueeze(1).broadcast_to([P, NT, SLOTS]), ALU.mult))
                        moe(dve.tensor_reduce(rc[:, 4, :], r1[:, :, :], AX.X, ALU.add))
                        early(4)
                        moe(dve.tensor_scalar(rc[:, 4, :], rc[:, 4, :], 0.2, 0.9, ALU.mult, ALU.add))
                        moe(dve.tensor_tensor(r2[:, :, :], r2[:, :, :], row(rc[:, 4, :]), ALU.mult))
                        moe.close()
                        for n in range(NT + 2):
                            if n < NT:
                                dve.wait_ge(*full_count(0, b, ("hU", n)))
                                if n >= 2:
                                    dve.wait_ge(*full_count(0, b, ("gT", n - 2)))
                                dve.tensor_tensor(gh[:, n % 2, :].rearrange("p (s r) -> p s r", s=SLOTS),
                                                  slot_of(0, ("hU", n)).rearrange("p (s r) -> p s r", s=SLOTS),
                                                  r2[:, n, :].unsqueeze(2).broadcast_to([P, SLOTS, RANK]),
                                                  ALU.mult).then_inc(free, 1)
                            for k in share(2 * n, 2 * NT + 4, EARLY):
                                row_maxima(0, k)
                            if n >= 2:
                                m = n - 2
                                dve.wait_ge(*full_count(0, b, ("ffn", m)))
                                if m == 0:
                                    dve.wait_ge(biased[0].sem, biased[0].count(b, 1))
                                dve.tensor_tensor(x[:, m, :], slot_of(0, ("ffn", m))[:, 0:D], x[:, m, :],
                                                  ALU.add).then_inc(free, 1)
                            if n < LATE:
                                project(NW - LATE + n)
                            for k in share(2 * n + 1, 2 * NT + 4, EARLY):
                                row_maxima(0, k)
                    else:
                        ff = Chain(dve, ff_chain, b)
                        for i in range(NT // 2):
                            dve.wait_ge(*full_count(1, b, ("ffn", i)))
                            if i == 0:
                                dve.wait_ge(biased[1].sem, biased[1].count(b, 1))
                            psum = slot_of(1, ("ffn", i)).rearrange("p (n d) -> p n d", n=2)
                            ff(dve.tensor_tensor(psum, psum, brow[:, 2, :].unsqueeze(1).broadcast_to([P, 2, D]), ALU.mult))
                            dve.tensor_tensor(x[:, 2 * i:2 * i + 2, :], psum, x[:, 2 * i:2 * i + 2, :],
                                              ALU.add).then_inc(free, 1)
                            for k in share_ff(2 * i):
                                row_maxima(0, k)
                            project(NW // 2 + i)
                            for k in share_ff(2 * i + 1):
                                row_maxima(0, k)
                        ff.close()
                        for n in range(NT - 1, -1, -1):
                            dve.wait_ge(*full_count(1, b, ("later", n)))
                            dve.tensor_copy(later_v[:, :].rearrange("p (h n c) -> p h n c", h=HEADS, n=NT)[:, :, n, :],
                                            slot_of(1, ("later", n))[:, 0:HEADS * VA].rearrange("p (h c) -> p h c", h=HEADS)
                                            ).then_inc(free, 1)
                            for k in share(NT - 1 - n, NT, WITH_FF):
                                row_maxima(0, k)

                    split_maxima(0)
                    for use in USES[NMX:]:
                        if l == 1 and use == ("out", NG - 1, 0):
                            next_link = input_moments(b.at(1))
                        ring_use(use)
                    if l == 1:
                        dve.wait_ge(st_full.sem, st_full.count(b.at(NG + 1), NEX))
                        normalise_input(next_link)
                    for i in range(NT // 2):
                        dve.wait_ge(*full_count(l, b, ("wo", i)))
                        dst = x if l == 0 else y
                        dve.tensor_tensor(dst[:, 2 * i:2 * i + 2, :], slot_of(l, ("wo", i)).rearrange("p (n d) -> p n d", n=2),
                                          x[:, 2 * i:2 * i + 2, :], ALU.add).then_inc(free, 1)
                        if l == 0 and i:
                            dve.wait_ge(*free_count(0, b, ("wo", i - 1)))
                            for n in (2 * i - 2, 2 * i - 1):
                                dve.bn_stats(stats[:, n, :], x[:, n, :])

        @block.tensor
        def _(pe):
            pe.wait_ge(w_in["first"], W_IN["first"])
            pe.matmul(ST[:, 0:SLOTS], waB[:, :], attrT[:, :], start=True, stop=True).then_inc(wz, 1)
            pe.wait_ge(wz_e, 1)
            pe.wait_ge(const_ok, CONST_OK)
            pe.wait_ge(w_in["qk"], W_IN["qk"])
            pe.sem_inc(pv_done.sem, pv_done.credit)

            with pe.Fori(0, B) as seq:
                b = Moment(pe, seq)
                for l in range(2):
                    turn = b.at(l)
                    full = unit_full[l].sem
                    L = str(l)

                    def unit(name):
                        i = names[l].index(name)
                        if i % NB4[l] >= 4:
                            pe.wait_ge(*free_count(l, b, names[l][i - 4]))
                        return slot_of(l, name)

                    def transposes(kind, src, i):
                        bank = unit((kind, i))
                        for c in range(KC):
                            for n in range(2):
                                mm = pe.transpose(bank[:, (2 * c + n) * P:(2 * c + n + 1) * P],
                                                  src[:, 2 * i + n, c * P:(c + 1) * P], ident[:, :])
                        mm.then_inc(full, 1)

                    def accumulate(dst, pairs):
                        for i, (lhsT, rhs) in enumerate(pairs):
                            mm = pe.matmul(dst, lhsT, rhs, start=(i == 0), stop=(i == len(pairs) - 1))
                        return mm

                    def tokens(weight, n):
                        return [(xT[:, c, n * P:(n + 1) * P], weight[:, c, :]) for c in range(KC)]

                    def wait_stacks(o):
                        pe.wait_ge(stacked[o].sem, stacked[o].count(turn, 2 * len(Q_PARTS)))

                    def bank_for(use):
                        pe.wait_ge(max_free.sem, max_free.count(turn, PLACE[use] - 1))
                        return bank_of(use)

                    def max_unit(g, i):
                        seg, qb, j, n, wd, diag = MAXU[i]
                        bank = bank_for(("max", g, i))
                        for k in range(n):
                            h = (g * GH + j + k) * T
                            q, c = h + qb * P, h + seg * 512
                            mm = pe.matmul(bank[:, k * wd:(k + 1) * wd], QS[0:KR, q:q + P], KS[0:KR, c:c + wd],
                                           start=True, stop=not diag)
                            if diag:
                                mm = pe.matmul(bank[:, (k + 1) * wd - P:(k + 1) * wd], identb[:, :], negmask[:, :], start=False, stop=True)
                        mm.then_inc(max_full.sem, 1)

                    if l == 0:
                        pe.wait_ge(unit_free[1, "dve"].sem, unit_free[1, "dve"].count(b, 0))
                    for i in range(NT // 2):
                        pe.wait_ge(normed[l].sem, normed[l].count(b, 2 * i + 2))
                        transposes("xT", xn0 if l == 0 else xn, i)
                    def project(c):
                        kind, ot, hf = chunk(c)
                        if ot == 0 and kind == "q":
                            pe.wait_ge(*free_count(l, b, ("xT", 2 * hf + 1)))
                        accumulate(unit((kind, ot, hf)),
                                   [(w[kind + L][:, i, ot * P:(ot + 1) * P], xT[:, i, hf * 512:(hf + 1) * 512])
                                    for i in range(KC)]).then_inc(full, 1)

                    for c in range(NW // 2):
                        project(c)
                    if l == 0:
                        pe.wait_ge(w_in["rest"], W_IN["rest"])
                        pe.wait_ge(wchain, WCHAIN)
                        bank = unit(("router", 0))
                        for n in range(NT):
                            mm = accumulate(bank[:, n * SLOTS:(n + 1) * SLOTS], tokens(w_r, n))
                        mm.then_inc(full, 1)
                    for i in range(NT // 2):
                        bank = unit(("v", i))
                        for n in range(2):
                            mm = accumulate(bank[:, n * D:(n + 1) * D], tokens(w["v" + L], 2 * i + n))
                        mm.then_inc(full, 1)
                    if l == 0:
                        for c in range(NW // 2, NW - LATE):
                            project(c)
                        for n in range(NT + 2):
                            if n < NT:
                                accumulate(unit(("hU", n)), tokens(w_u, n)).then_inc(full, 1)
                            if n == 0:
                                wait_stacks(0)
                                for i in range(EARLY):
                                    max_unit(0, i)
                            for i in share(2 * n, 2 * NT + 4, EARLY):
                                max_unit(0, i)
                            if 1 <= n <= NT:
                                m = n - 1
                                pe.wait_ge(*free_count(0, b, ("hU", m)))
                                bank = unit(("gT", m))
                                for c in range(FC):
                                    mm = pe.transpose(bank[:, c * P:(c + 1) * P], gh[:, m % 2, c * P:(c + 1) * P], ident[:, :])
                                mm.then_inc(full, 1)
                            if n >= 2:
                                m = n - 2
                                pe.wait_ge(*free_count(0, b, ("gT", m)))
                                accumulate(unit(("ffn", m))[:, 0:D],
                                           [(ghT[:, m % 2, c, :], w_v[:, c, :]) for c in range(FC)]).then_inc(full, 1)
                            if n < LATE:
                                project(NW - LATE + n)
                            for i in share(2 * n + 1, 2 * NT + 4, EARLY):
                                max_unit(0, i)
                    else:
                        for i in range(NT // 2):
                            pe.wait_ge(normed2.sem, normed2.count(b, 2 * i + 2))
                            transposes("x2T", xn, i)
                        for i in range(NT // 2):
                            pe.wait_ge(*free_count(1, b, ("x2T", i)))
                            bank = unit(("ffn", i))
                            for n in range(2):
                                t0 = (2 * i + n) * P
                                mm = accumulate(bank[:, n * D:(n + 1) * D],
                                                [(x2T[:, c, t0:t0 + P], w["f1"][:, c, :]) for c in range(KC)])
                            mm.then_inc(full, 1)
                            if i == 0:
                                wait_stacks(0)
                            for k in share_ff(2 * i):
                                max_unit(0, k)
                            project(NW // 2 + i)
                            for k in share_ff(2 * i + 1):
                                max_unit(0, k)
                        Vt = Vaug[:, :].rearrange("p (n c) -> p n c", n=NT)
                        pe.wait_ge(*free_count(1, b, ("v", NT // 2 - 1)))
                        for n in range(NT - 1, -1, -1):
                            bank = unit(("later", n))[:, 0:HEADS * VA]
                            pairs = [(strict[:, :], Vt[:, n, :])]
                            if n == 6:
                                pairs += [(ones[:, :], Vt[:, 7, :])]
                            elif n < 6:
                                pe.wait_ge(suffix_ok.sem, suffix_ok.count(b, 6 - n))
                                pairs += [(ones[:, :], suffix[:, n, :])]
                            accumulate(bank, pairs).then_inc(full, 1)
                            for k in share(NT - 1 - n, NT, WITH_FF):
                                max_unit(0, k)

                    if l == 0:
                        pe.wait_ge(*free_count(0, b, ("v", NT // 2 - 1)))
                    def transpose_maxima(g):
                        bank = bank_for(("rows", g)).bitcast(BF16)
                        pe.wait_ge(negmax_parts.sem, negmax_parts.count(b.at(l * NG + g), 1))
                        pe.transpose(bank[0:3 * GH * NT, 0:P], nmp[:, :, :].rearrange("p a c -> p (a c)"),
                                     identb[:, :]).then_inc(max_full.sem, 1)

                    def st_unit(g, u):
                        kb, j, n = EXPU[u]
                        wd = T - kb * P
                        pe.wait_ge(exp_done.sem, exp_done.count(b.at(l * NG + g), u - 1))
                        for k in range(n):
                            h = (g * GH + j + k) * T + kb * P
                            o = (u % 2) * 1024 + k * (wd if n != 2 else 512)
                            for q0 in range(0, wd, 512):
                                qw = min(512, wd - q0)
                                mm = pe.matmul(ST[:, o + q0:o + q0 + qw], KS[0:KM, h:h + P], QS[0:KM, h + q0:h + q0 + qw],
                                               start=True, stop=q0 > 0)
                                if q0 == 0:
                                    mm = pe.matmul(ST[:, o:o + P], identb[:, :], negmaskT[:, :], start=False, stop=True)
                        mm.then_inc(st_full.sem, 1)

                    def pv(g, kb, half):
                        G = b.at(l * NG + g)
                        last = max(i for i, e in enumerate(EXPU) if e[0] == kb)
                        pe.wait_ge(exp_done.sem, exp_done.count(G, last + 1))
                        if kb == 0:
                            pe.wait_ge(o_copied.sem, o_copied.count(G, half - 1))
                        q0, q1 = max(kb * P, half * 512), (half + 1) * 512
                        for j in range(GH):
                            v0 = (kb * HEADS + g * GH + j) * VA
                            mm = pe.matmul(O[32 * j:32 * j + VA, q0:q1], Vaug[:, v0:v0 + VA],
                                           PT[:, kb % 2, j, q0 - kb * P:q1 - kb * P],
                                           start=(kb == 0), stop=(kb == 4 * half + 3), tile_position=(0, 32 * j))
                        if half:
                            mm.then_inc(pv_done.sem, 1)

                    def turn_outputs(g, t):
                        bank = bank_for(("out", g, t))
                        pe.wait_ge(o_copied.sem, o_copied.count(b.at(l * NG + g), t + 1))
                        for n in range(4):
                            mm = pe.transpose(bank[:, n * P:(n + 1) * P], OT[:, (4 * t + n) * P:(4 * t + n + 1) * P], ident[:, :])
                        mm.then_inc(max_full.sem, 1)

                    run = {"st": st_unit, "pv": pv, "max": max_unit, "rows": transpose_maxima, "out": turn_outputs}

                    def step(kind, *what):
                        run[kind](*what)

                    for c in ("act", "dve"):
                        s = unit_free[l, c]
                        pe.wait_ge(s.sem, s.count(b, sum(e == c for _, e in US[l][:NB4[l]])))
                    wait_stacks(1)
                    for what in ORDER:
                        if what[0] == "st" and what[2] == 0:
                            pe.wait_ge(negmax_in.sem, negmax_in.count(b.at(l * NG + what[1]), 1))
                        step(*what)

                    pe.wait_ge(max_free.sem, max_free.count(turn, RING_TURN))
                    for i in range(NT // 2 + 1):
                        if i < NT // 2:
                            transposes("aT", attn, i)
                        if i >= 1:
                            m = i - 1
                            pe.wait_ge(*free_count(l, b, ("aT", m)))
                            bank = unit(("wo", m))
                            for n in range(2):
                                t0 = (2 * m + n) * P
                                mm = accumulate(bank[:, n * D:(n + 1) * D],
                                                [(attnT[:, c, t0:t0 + P], w["o" + L][:, c, :]) for c in range(KC)])
                            mm.then_inc(full, 1)


WCHAIN = 7
MOE_EXP_AT = 16
MOE_STEPS = 27


def tables():
    half = DH // 2
    inv = (np.float32(1.0) / np.power(np.float32(10000.0), np.arange(half, dtype=np.float32) / np.float32(half))).astype(np.float32)
    freqs = np.arange(T, dtype=np.float32)[None, :] * inv[:, None]
    cos = np.repeat(np.cos(freqs), HC, axis=0).astype(np.float32)
    sin = np.repeat(np.sin(freqs), HC, axis=0).astype(np.float32)
    return np.concatenate([cos, cos]), np.concatenate([sin, -sin])


def columns(*vectors):
    return np.stack([v.reshape(KC, P).T for v in vectors], axis=1)


def kernel(**inputs):
    import concourse.bacc as _bacc
    from concourse.bass_utils import run_bass_kernel_spmd as _run

    i = {n: np.asarray(v) for n, v in inputs.items()}
    cols = np.arange(D).reshape(KC, HC, DH // 2, 2).transpose(0, 3, 2, 1).ravel()
    cos, sin = tables()
    arrays = {
        "x": np.concatenate([i["L0_attn_x"], i["L0_attn_x"][-1:]]),
        "w_q0": i["L0_attn_Wq"][cols].T, "w_k0": i["L0_attn_Wk"][cols].T,
        "w_v0": i["L0_attn_Wv"].T, "w_o0": i["L0_attn_Wo"].T,
        "w_q1": i["L1_attn_Wq"][:, cols], "w_k1": i["L1_attn_Wk"][:, cols], "w_v1": i["L1_attn_Wv"], "w_o1": i["L1_attn_Wo"],
        "w_f1": i["L1_ffn_weight"].T,
        "bcol": columns(i["L0_attn_bq"][cols], i["L0_attn_bk"][cols]),
        "lncol": columns(i["L1_ffn_ln_weight"], i["L1_ffn_ln_bias"]),
        "bv": i["L0_attn_bv"], "bo": i["L0_attn_bo"],
        "w_r": i["L0_ffn_Wr"].T,
        "w_u": i["L0_ffn_U"].transpose(1, 0, 2).reshape(D, FF),
        "w_v": i["L0_ffn_V"].reshape(FF, D),
        "attrT": i["L0_ffn_attr"].T, "waB": np.tile(i["L0_ffn_Wa"].T, (1, P)),
        "gamma": i["L1_ffn_gamma"], "beta": i["L1_ffn_beta"],
        "cos": cos, "sin": sin,
    }
    nc = _bacc.Bacc("TRN2", target_bir_lowering=False, num_devices=1)
    feeds, aps = {}, {}
    for n, v in arrays.items():
        v = np.ascontiguousarray(v)
        feeds[f"in_{n}"] = v
        aps[n] = nc.dram_tensor(f"in_{n}", v.shape, mybir.dt.from_np(v.dtype), kind="ExternalInput").ap()
    out = nc.dram_tensor("out", (B, T, D), F32, kind="ExternalOutput").ap()
    build(nc, aps, out)
    r = _run(nc, [feeds], core_ids=[0])
    return r.results[0]["out"]
```
